# Optimizing a Trainium2 kernel written in Bass

```python
import numpy as np
import jax
import jax.numpy as jnp

def _softmax(x, axis=-1):
    return jax.nn.softmax(x, axis=axis)

def _gelu(x):
    return jax.nn.gelu(x, approximate=True)

def _silu(x):
    return jax.nn.silu(x)

def _sigmoid(x):
    return jax.nn.sigmoid(x)

def _layernorm(x, axis=-1, eps=1e-05):
    m = jnp.mean(x, axis=axis, keepdims=True)
    v = jnp.var(x, axis=axis, keepdims=True)
    return (x - m) / jnp.sqrt(v + eps)

def _scatter_add(tgt, idx, src, axis=0):
    return tgt.at[idx].add(src)

def _segment_sum(src, seg, n):
    return jax.ops.segment_sum(src, seg, n)
kernel_name = 'mk_adj_resnorm_d2_adj_r2_fa58e3'

def setup_inputs(seed: int=0):
    np.random.seed(seed)
    _w = jnp.asarray

    def _rec_inputs():
        import jax
        import jax.numpy as jnp
        _gk = jax.random.key(seed)
        x = -0.000125 + 0.9999 * jax.random.normal(jax.random.fold_in(_gk, 1), (128, 128, 128), jnp.float32)
        _w = (1.0 + jnp.arange(128, dtype=jnp.float32)) ** (-0.5)
        _w = _w / _w.mean()
        _pij = jnp.clip(0.0625 * _w[:, None] * _w[None, :], 0.0, 1.0)
        _a = jax.random.uniform(jax.random.fold_in(_gk, 2), (128, 128)) < _pij
        _a = jnp.logical_or(_a, jnp.swapaxes(_a, -1, -2))
        _a = jnp.logical_or(_a, jnp.eye(128, dtype=bool))
        _af = _a.astype(jnp.float32)
        _af = _af * jax.random.uniform(jax.random.fold_in(_gk, 3), (128, 128), jnp.float32, 0.05, 0.000488281)
        adj = _af
        return (x, adj)
    x, adj = _rec_inputs()

    def _L0_gnn_setup():
        import jax, jax.numpy as jnp
        import numpy as np
        B, T, D, H = (64, 1024, 128, 128)
        MAX_SKIP = 4

        def _lstm_last(Wih, Whh, bih, bhh, xs):
            N, _, Hd = xs.shape
            bias = bih + bhh

            def step(carry, x_t):
                h, c = carry
                g = x_t @ Wih.T + h @ Whh.T + bias
                i, f, gg, o = jnp.split(g, 4, axis=-1)
                c = jax.nn.sigmoid(f) * c + jax.nn.sigmoid(i) * jnp.tanh(gg)
                h = jax.nn.sigmoid(o) * jnp.tanh(c)
                return ((h, c), None)
            init = (jnp.zeros((N, Hd), xs.dtype), jnp.zeros((N, Hd), xs.dtype))
            (h_last, _), _ = jax.lax.scan(step, init, jnp.swapaxes(xs, 0, 1))
            return h_last
        key = jax.random.key(seed)
        ks = jax.random.split(key, 8)
        s = 0.05
        x = jax.random.normal(ks[0], (B, T, D), jnp.float32)
        adj = jax.random.uniform(ks[1], (T, T), jnp.float32) / T
        Wg0 = jax.random.normal(ks[2], (D, H), jnp.float32) * s
        bg0 = jnp.zeros((H,), jnp.float32)
        Wg1 = jax.random.normal(ks[3], (H, H), jnp.float32) * s
        bg1 = jnp.zeros((H,), jnp.float32)
        Wih = jax.random.normal(ks[4], (MAX_SKIP, 4 * H, H), jnp.float32) * s
        Whh = jax.random.normal(ks[5], (MAX_SKIP, 4 * H, H), jnp.float32) * s
        bih = jax.random.normal(ks[6], (MAX_SKIP, 4 * H), jnp.float32) * s
        bhh = jax.random.normal(ks[7], (MAX_SKIP, 4 * H), jnp.float32) * s
        return dict(x=x, adj=adj, Wg0=Wg0, bg0=bg0, Wg1=Wg1, bg1=bg1, Wih=Wih, Whh=Whh, bih=bih, bhh=bhh)
    _L0_gnn_all = _L0_gnn_setup()
    _L0_gnn_in = {k: v for k, v in _L0_gnn_all.items() if k in ('Wg0', 'bg0', 'Wg1', 'bg1', 'Wih', 'Whh', 'bih', 'bhh')}
    del _L0_gnn_all

    def _L1_gnn_setup():
        import jax, jax.numpy as jnp
        import numpy as np
        EPS = 1e-05

        def _batchnorm(x, gamma, beta):
            mu = jnp.mean(x, axis=0)
            var = jnp.var(x, axis=0)
            return (x - mu) * jax.lax.rsqrt(var + EPS) * gamma + beta
        key = jax.random.key(seed)
        ks = jax.random.split(key, 4)
        b, n, d, h, o = (32, 1024, 128, 256, 128)
        features = jax.random.normal(ks[0], (b, n, d), dtype=jnp.float32)
        A = jax.random.uniform(ks[1], (n, n), dtype=jnp.float32)
        lim1 = float(np.sqrt(6.0 / (d + h)))
        W1 = jax.random.uniform(ks[2], (h, d), minval=-lim1, maxval=lim1, dtype=jnp.float32)
        b1 = jnp.zeros((h,), jnp.float32)
        lim2 = float(np.sqrt(6.0 / (h + o)))
        W2 = jax.random.uniform(ks[3], (o, h), minval=-lim2, maxval=lim2, dtype=jnp.float32)
        b2 = jnp.zeros((o,), jnp.float32)
        g1 = jnp.ones((h,), jnp.float32)
        be1 = jnp.zeros((h,), jnp.float32)
        g2 = jnp.ones((o,), jnp.float32)
        be2 = jnp.zeros((o,), jnp.float32)
        return {'features': features, 'A': A, 'W1': W1, 'b1': b1, 'g1': g1, 'be1': be1, 'W2': W2, 'b2': b2, 'g2': g2, 'be2': be2}
    _L1_gnn_all = _L1_gnn_setup()
    _L1_gnn_in = {k: v for k, v in _L1_gnn_all.items() if k in ('W1', 'b1', 'g1', 'be1', 'W2', 'b2', 'g2', 'be2')}
    del _L1_gnn_all
    return {'x': x, 'adj': adj, 'L0_gnn_Wg0': _L0_gnn_in['Wg0'], 'L0_gnn_bg0': _L0_gnn_in['bg0'], 'L0_gnn_Wg1': _L0_gnn_in['Wg1'], 'L0_gnn_bg1': _L0_gnn_in['bg1'], 'L0_gnn_Wih': _L0_gnn_in['Wih'], 'L0_gnn_Whh': _L0_gnn_in['Whh'], 'L0_gnn_bih': _L0_gnn_in['bih'], 'L0_gnn_bhh': _L0_gnn_in['bhh'], 'L1_gnn_W1': _L1_gnn_in['W1'], 'L1_gnn_b1': _L1_gnn_in['b1'], 'L1_gnn_g1': _L1_gnn_in['g1'], 'L1_gnn_be1': _L1_gnn_in['be1'], 'L1_gnn_W2': _L1_gnn_in['W2'], 'L1_gnn_b2': _L1_gnn_in['b2'], 'L1_gnn_g2': _L1_gnn_in['g2'], 'L1_gnn_be2': _L1_gnn_in['be2']}

def reference(x, adj, L0_gnn_Wg0, L0_gnn_bg0, L0_gnn_Wg1, L0_gnn_bg1, L0_gnn_Wih, L0_gnn_Whh, L0_gnn_bih, L0_gnn_bhh, L1_gnn_W1, L1_gnn_b1, L1_gnn_g1, L1_gnn_be1, L1_gnn_W2, L1_gnn_b2, L1_gnn_g2, L1_gnn_be2):
    import jax
    import jax.numpy as jnp

    def _L0_gnn_ref(x, adj, Wg0, bg0, Wg1, bg1, Wih, Whh, bih, bhh):
        import jax, jax.numpy as jnp
        import numpy as np
        B, T, D, H = (64, 1024, 128, 128)
        MAX_SKIP = 4

        def _lstm_last(Wih, Whh, bih, bhh, xs):
            N, _, Hd = xs.shape
            bias = bih + bhh

            def step(carry, x_t):
                h, c = carry
                g = x_t @ Wih.T + h @ Whh.T + bias
                i, f, gg, o = jnp.split(g, 4, axis=-1)
                c = jax.nn.sigmoid(f) * c + jax.nn.sigmoid(i) * jnp.tanh(gg)
                h = jax.nn.sigmoid(o) * jnp.tanh(c)
                return ((h, c), None)
            init = (jnp.zeros((N, Hd), xs.dtype), jnp.zeros((N, Hd), xs.dtype))
            (h_last, _), _ = jax.lax.scan(step, init, jnp.swapaxes(xs, 0, 1))
            return h_last
        h = jax.nn.relu(jnp.einsum('ts,bsh->bth', adj, x @ Wg0 + bg0))
        h = jax.nn.relu(jnp.einsum('ts,bsh->bth', adj, h @ Wg1 + bg1))
        Bv, Tv, Hd = h.shape
        for p in range(1, MAX_SKIP + 1):
            nw = Tv // p
            wins = h[:, :nw * p, :].reshape(Bv * nw, p, Hd)
            last = _lstm_last(Wih[p - 1], Whh[p - 1], bih[p - 1], bhh[p - 1], wins)
            idx = jnp.arange(nw) * p + (p - 1)
            h = h.at[:, idx, :].set(last.reshape(Bv, nw, Hd))
        return h

    def _L1_gnn_ref(features, A, W1, b1, g1, be1, W2, b2, g2, be2):
        import jax, jax.numpy as jnp
        import numpy as np
        EPS = 1e-05

        def _batchnorm(x, gamma, beta):
            mu = jnp.mean(x, axis=0)
            var = jnp.var(x, axis=0)
            return (x - mu) * jax.lax.rsqrt(var + EPS) * gamma + beta
        b, n, d = features.shape
        A_norm = A + jnp.eye(n, dtype=A.dtype)
        deg = jnp.sum(A_norm, axis=0) + jnp.sum(A_norm, axis=1) - jnp.diagonal(A_norm)
        dinv = jax.lax.rsqrt(deg)
        A_hat = A_norm * dinv[:, None] * dinv[None, :]
        agg = jnp.einsum('nm,bmd->bnd', A_hat, features)
        x = agg.reshape(-1, d)
        h = jax.nn.relu(_batchnorm(x @ W1.T + b1, g1, be1))
        out = h @ W2.T + b2
        out = _batchnorm(out, g2, be2)
        return out.reshape(b, n, -1)
    x = _layernorm(x + _L0_gnn_ref(x, adj, L0_gnn_Wg0, L0_gnn_bg0, L0_gnn_Wg1, L0_gnn_bg1, L0_gnn_Wih, L0_gnn_Whh, L0_gnn_bih, L0_gnn_bhh), axis=-1)
    x = _layernorm(x + _L1_gnn_ref(x, adj, L1_gnn_W1, L1_gnn_b1, L1_gnn_g1, L1_gnn_be1, L1_gnn_W2, L1_gnn_b2, L1_gnn_g2, L1_gnn_be2), axis=-1)
    return x

_drawn_inputs = setup_inputs


def setup_inputs(seed=0):
    import zlib

    import numpy as np

    out = dict(_drawn_inputs(seed))
    spreads = {'L0_gnn_bg0': (0.0, 0.8),
     'L0_gnn_bg1': (0.0, 0.8),
     'L1_gnn_b1': (0.0, 0.8),
     'L1_gnn_g1': (1.0, 0.2),
     'L1_gnn_be1': (0.0, 0.1),
     'L1_gnn_b2': (0.0, 0.8),
     'L1_gnn_g2': (1.0, 0.2),
     'L1_gnn_be2': (0.0, 0.1)}
    factors = {'L0_gnn_Wg0': 8.0,
     'L0_gnn_Wg1': 8.0,
     'L0_gnn_Wih': 7.17,
     'L0_gnn_Whh': 8.0,
     'L0_gnn_bih': 2.795,
     'L0_gnn_bhh': 2.813}
    for name, (base, spread) in spreads.items():
        noise = np.random.default_rng([zlib.crc32(name.encode()), seed]).standard_normal(out[name].shape)
        drawn = base * np.exp(spread * noise) if base else spread * noise
        out[name] = jnp.asarray(drawn.astype(out[name].dtype))
    for name, factor in factors.items():
        out[name] = (out[name] * factor).astype(out[name].dtype)
    return out
```

```python
from contextlib import ExitStack

import numpy as np

import concourse.bass as bass
from concourse import mybir

F32 = mybir.dt.float32
F16 = mybir.dt.float16
ALU = mybir.AluOpType
ACT = mybir.ActivationFunctionType

P = 128
BANK = 512
EPS = 1e-5
GB = 8
SKIPS = (2, 3, 4)
W_SCALE = 2.0 ** 6
H_SCALE = 2.0 ** 14
GATES_FIRST = ("i", "g", "o")
GATES_NEXT = ("i", "g", "f", "o")
GATE_AT = {"i": 0, "f": 1, "g": 2, "o": 3}

START = {"z_stored": 1, "z_stats": 1}

LSTM_JOBS = [("lstm", 1, c) for c in range(2)] + [("lstm", p, k) for p in SKIPS for k in range(p)]
JOBS = [("mix0",), ("lin0",), ("lin1",), ("mix1",)] + LSTM_JOBS + [("norm",), ("agg",), ("z1",)]


def gates_of(job):
    return GATES_FIRST if job[1] == 1 or job[2] == 0 else GATES_NEXT


def count_signals():
    total, at = {}, {}

    def signal(sem, key):
        total[sem] = total.get(sem, 0) + 1
        at[sem, key] = total[sem]

    for job in JOBS:
        kind = job[0]
        if kind == "lstm":
            for g in gates_of(job):
                signal("gates_full", (job, g))
                signal("gate_ready", (job, g))
            signal("tanh_cell", job)
            for what in ("input", "kept", "cell") if "f" in gates_of(job) else ("cell",):
                signal("cell_part", (job, what))
            for what in ("h", "high", "low"):
                signal("hidden", (job, what))
            continue
        for n in range(4 if kind == "z1" else 2):
            signal("product_full", (job, n))
        if kind in ("mix0", "lin0", "mix1", "agg"):
            for n in range(2):
                signal("evacuated", (job, n))
        if kind in ("lin0", "lin1"):
            for n in range(2):
                signal("biased", (job, n))
        if kind == "norm":
            for n in range(2):
                signal("residual", n)
            for n in range(1, 5):
                signal("moments", n)
            signal("rstd", 0)
            signal("normed", 0)
        if kind == "z1":
            for n in range(4):
                signal("z_stored", n)
            signal("z_stats", "bn")
            signal("z_stats", "kept")
    return total, at


def gnn_lstm_kernel(nc, x, adj, adjT, w0, b0_rep, w1, b1_rep, wih1, b_ih, b_hh, wr, gw1, gw2, vec1, vec2, out):
    NB = x.shape[0] * GB
    HALVES = x.shape[0]
    GROUPS = HALVES // 2
    HW = GB * P
    CHUNKS = HALVES * 2
    PER, AT = count_signals()

    x1_dram = nc.dram_tensor("x1_kept", [HALVES, P, HW], F32, kind="Internal").ap()

    with ExitStack() as ctx:
        def sb(name, shape, dt=F32):
            return ctx.enter_context(nc.sbuf_tensor(name, shape, dt))

        def sem(name):
            return ctx.enter_context(nc.semaphore(name))

        adj_sb = sb("adj_sb", [P, P])
        adjT_sb = sb("adjT_sb", [P, P])
        ahatT = sb("ahatT", [P, P])
        ident = sb("ident", [P, P])
        ident16 = sb("ident16", [P, P], F16)
        w0_sb = sb("w0_sb", [P, P])
        w1_sb = sb("w1_sb", [P, P])
        bias0 = sb("bias0", [P, P])
        bias1 = sb("bias1", [P, P])
        wih1_sb = sb("wih1_sb", [P, 3, P])
        w_hi = sb("w_hi", [P, len(SKIPS), 2, 4 * P], F16)
        w_lo = sb("w_lo", [P, len(SKIPS), 2, 4 * P], F16)
        lstm_bias = sb("lstm_bias", [P, 4, 4])
        bhh_sb = sb("bhh_sb", [P, 4, 4])
        gw1_sb = sb("gw1_sb", [P, 2, P])
        gw2_sb = sb("gw2_sb", [P, 2, P])
        v1_sb = sb("v1_sb", [P, 3, 2])
        v2_sb = sb("v2_sb", [P, 3])
        small = sb("small", [P, 16])
        neg_half = sb("neg_half", [P, GB])

        z = sb("z", [P, CHUNKS, 2, BANK])
        z_moments = sb("z_moments", [P, 2, CHUNKS, 6])

        def two(name, shape, dt=F32):
            return [sb(f"{name}{h}", shape, dt) for h in range(2)]

        xin = two("xin", [P, GB, P])
        buf1 = two("buf1", [P, 2, BANK])
        buf2 = two("buf2", [P, 2, BANK])
        h_hi = two("h_hi", [P, GB, P], F16)
        h_lo = two("h_lo", [P, GB, P], F16)
        s_hi = two("s_hi", [P, BANK], F16)
        s_lo = two("s_lo", [P, BANK], F16)
        gate_f = two("gate_f", [P, BANK])
        gate_o = two("gate_o", [P, BANK])
        cell = two("cell", [P, BANK])
        tcell = two("tcell", [P, BANK])
        bn = two("bn", [P, GB, 6])
        comb = two("comb", [P, 3, GB])
        mv = sb("mv", [P, 2, 2])
        veps = two("veps", [P, GB])
        rstd = two("rstd", [P, GB])
        zbn = two("zbn", [P, 2, 2, 6])
        gate_i = [buf1[h][:, 0, :] for h in range(2)]
        gate_g = [buf1[h][:, 1, :] for h in range(2)]
        acts = {"i": gate_i, "g": gate_g, "f": [t[:] for t in gate_f], "o": [t[:] for t in gate_o]}
        w_stage = z[:, 0:len(SKIPS), :, :]

        bank = [[ctx.enter_context(nc.psum_tensor(f"bank{h}{n}", [P, BANK], F32)) for n in range(4)]
                for h in range(2)]

        sem_loaded = sem("weights_loaded")
        sem_ident = sem("ident_ready")
        sem_setup = sem("setup_step")
        sem_degree = sem("degree_step")
        sem_setup_pe = sem("setup_product")
        sem_setup_pool = sem("setup_pow")
        sem_x = [sem(f"x_loaded{h}") for h in range(2)]
        sem_kept = [sem(f"x1_kept{h}") for h in range(2)]
        S = {name: [sem(f"{name}{h}") for h in range(2)] for name in PER}
        sem_bn1 = sem("bn1_step")
        sem_bn1_pow = sem("bn1_pow")
        r_ready = [sem(f"r_ready{h}") for h in range(2)]
        z2_full = [sem(f"z2_full{h}") for h in range(2)]
        z2_bn = [sem(f"z2_bn{h}") for h in range(2)]
        z2_kept = [sem(f"z2_kept{h}") for h in range(2)]
        sem_bn2 = sem("bn2_step")
        sem_bn2_pow = sem("bn2_pow")
        y_scaled = [sem(f"y_scaled{h}") for h in range(2)]
        z2_moments = [sem(f"z2_moments{h}") for h in range(2)]
        x1_back = [sem(f"x1_back{h}") for h in range(2)]
        y_full = [sem(f"y_full{h}") for h in range(2)]
        y_res = [sem(f"y_res{h}") for h in range(2)]
        y_mom = [sem(f"y_moments{h}") for h in range(2)]
        y_rstd = [sem(f"y_rstd{h}") for h in range(2)]
        y_norm = [sem(f"y_normed{h}") for h in range(2)]
        y_out = [sem(f"y_stored{h}") for h in range(2)]

        def wait(eng, name, h, g, key):
            eng.wait_ge(S[name][h], g * PER[name] + AT[name, key] + START.get(name, 0))

        def wait_last(eng, name, h, g):
            eng.wait_ge(S[name][h], g * PER[name] + START[name])

        free_at_start = [sem_kept, z2_bn, z2_kept, y_full, y_res, y_out] + [S[n] for n in START]

        def order():
            return [(h, job) for job in JOBS for h in range(2)]

        LOADS = 14
        block = ctx.enter_context(nc.Block())

        @block.sync
        def _(sp):
            for h in range(2):
                sp.dma_start(xin[h][:].rearrange("p b d -> p (b d)"), x[h]).then_inc(sem_x[h], 16)
            for dst, src in (
                (adjT_sb[:], adjT), (adj_sb[:], adj), (w0_sb[:], w0), (bias0[:], b0_rep), (w1_sb[:], w1),
                (bias1[:], b1_rep), (wih1_sb[:], wih1), (lstm_bias[:], b_ih), (bhh_sb[:], b_hh),
                (w_stage, wr), (gw1_sb[:], gw1), (gw2_sb[:], gw2), (v1_sb[:], vec1), (v2_sb[:], vec2),
            ):
                sp.dma_start(dst, src).then_inc(sem_loaded, 16)

            def keep_x1(h, g):
                wait(sp, "normed", h, g, 0)
                sp.dma_start(x1_dram[bass.ds(2 * g + h, 1)].rearrange("o p n -> p (o n)"),
                             buf2[h][:].rearrange("p a b -> p (a b)")).then_inc(sem_kept[h], 16)

            with sp.Fori(0, GROUPS - 1) as g:
                for h in range(2):
                    wait(sp, "residual", h, g, 1)
                    sp.dma_start(xin[h][:].rearrange("p b d -> p (b d)"),
                                 x[bass.ds(2 * g + 2 + h, 1)].rearrange("o p n -> p (o n)")).then_inc(sem_x[h], 16)
                for h in range(2):
                    keep_x1(h, g)
            for h in range(2):
                keep_x1(h, GROUPS - 1)

            for h in range(2):
                sp.wait_ge(sem_kept[h], 16 * GROUPS + 1)
            for h in range(2):
                sp.dma_start(xin[h][:].rearrange("p b d -> p (b d)"), x1_dram[h]).then_inc(x1_back[h], 16)

            def store(h, g):
                sp.wait_ge(y_norm[h], g + 1)
                sp.dma_start(out[bass.ds(2 * g + h, 1)].rearrange("o p n -> p (o n)"),
                             buf2[h][:].rearrange("p a b -> p (a b)")).then_inc(y_out[h], 16)

            with sp.Fori(0, GROUPS - 1) as g:
                for h in range(2):
                    sp.wait_ge(y_res[h], 2 * g + 3)
                    sp.dma_start(xin[h][:].rearrange("p b d -> p (b d)"),
                                 x1_dram[bass.ds(2 * g + 2 + h, 1)].rearrange("o p n -> p (o n)")
                                 ).then_inc(x1_back[h], 16)
                    store(h, g)
            for h in range(2):
                store(h, GROUPS - 1)
            for h in range(2):
                sp.wait_ge(y_out[h], 16 * GROUPS + 1)

        @block.gpsimd
        def _(pool):
            for pair in free_at_start:
                for s in pair:
                    pool.sem_inc(s, 1)
            nc.gpsimd.memset(ident[:], 0.0).then_inc(sem_ident, 1)
            nc.gpsimd.memset(neg_half[:], -0.5).then_inc(sem_ident, 1)
            pool.wait_ge(sem_ident, 2)
            nc.gpsimd.affine_select(out=ident[:], in_=ident[:], compare_op=ALU.not_equal, fill=1.0, base=0,
                                    pattern=[[-1, P]], channel_multiplier=1).then_inc(sem_ident, 1)
            pool.wait_ge(sem_setup, 2)
            nc.gpsimd.tensor_tensor(small[:, 3:4], small[:, 2:3], neg_half[:, 0:1], ALU.pow).then_inc(sem_setup_pool, 1)
            with pool.Fori(0, GROUPS) as g:
                for h in range(2):
                    wait(pool, "moments", h, g, 4)
                    nc.gpsimd.tensor_tensor(rstd[h][:], veps[h][:], neg_half[:], ALU.pow).then_inc(S["rstd"][h], 1)
            pool.wait_ge(sem_bn1, 2)
            nc.gpsimd.tensor_tensor(small[:, 6:8], small[:, 4:6], neg_half[:, 0:2], ALU.pow).then_inc(sem_bn1_pow, 1)
            pool.wait_ge(sem_bn2, 2)
            nc.gpsimd.tensor_tensor(small[:, 13:14], small[:, 12:13], neg_half[:, 0:1], ALU.pow).then_inc(sem_bn2_pow, 1)
            with pool.Fori(0, GROUPS) as g:
                for h in range(2):
                    pool.wait_ge(y_mom[h], 4 * g + 4)
                    nc.gpsimd.tensor_tensor(rstd[h][:], veps[h][:], neg_half[:], ALU.pow).then_inc(y_rstd[h], 1)

        def window(t, p, k):
            nw = P // p
            return t[:, :, k:k + p * (nw - 1) + 1:p]

        def lstm_bank(job, n):
            return (n + 3) % 4 if job == ("lstm", 1, 1) else n

        @block.tensor
        def _(pe):
            mm = nc.tensor.matmul
            pe.wait_ge(sem_loaded, 16 * LOADS)
            pe.wait_ge(sem_ident, 3)
            pe.wait_ge(sem_setup, 3)
            mm(bank[0][0][:, 0:P], bias0[:], adjT_sb[:], start=True, stop=True).then_inc(sem_setup_pe, 1)
            mm(bank[0][1][:, 0:P], adj_sb[:], buf2[0][:, 0, 0:P], start=True, stop=True).then_inc(sem_setup_pe, 1)
            pe.wait_ge(sem_setup, 6)

            def mix(h, job, g, banks, lhs, rhs, ready):
                for n in range(2):
                    ready(n)
                    for b in range(4 * n, 4 * n + 4):
                        last = mm(bank[h][banks[n]][:, (b % 4) * P:(b % 4 + 1) * P], lhs(b), rhs,
                                  start=True, stop=True)
                    last.then_inc(S["product_full"][h], 1)

            def emit(h, job, g):
                b1 = buf1[h][:].rearrange("p a (b n) -> p (a b) n", n=P)
                b2 = buf2[h][:].rearrange("p a (b n) -> p (a b) n", n=P)
                kind = job[0]
                if kind == "mix0":
                    pe.wait_ge(sem_x[h], 16 * g + 16)
                    wait_last(pe, "z_stored", h, g)
                    wait_last(pe, "z_stats", h, g)
                    mix(h, job, g, (0, 1), lambda b: xin[h][:, b, :], adjT_sb[:], lambda n: None)
                elif kind == "lin0":
                    for n in range(2):
                        wait(pe, "evacuated", h, g, (("mix0",), n))
                        mm(bank[h][2 + n][:], w0_sb[:], buf1[h][:, n, :], start=True, stop=True
                           ).then_inc(S["product_full"][h], 1)
                elif kind == "lin1":
                    mix(h, job, g, (0, 1), lambda b: b2[:, b, :], w1_sb[:],
                        lambda n: wait(pe, "evacuated", h, g, (("lin0",), n)))
                elif kind == "mix1":
                    mix(h, job, g, (2, 3), lambda b: b1[:, b, :], adjT_sb[:],
                        lambda n: wait(pe, "biased", h, g, (("lin1",), n)))
                elif kind == "lstm" and job[1] == 1:
                    c = job[2]
                    wait(pe, "evacuated", h, g, (("mix1",), c))
                    for n, gate in enumerate(GATES_FIRST):
                        if c == 1 and n > 0:
                            wait(pe, "gate_ready", h, g, (("lstm", 1, 0), GATES_FIRST[n - 1]))
                        mm(bank[h][lstm_bank(job, n)][:], wih1_sb[:, n, :], buf2[h][:, c, :], start=True, stop=True
                           ).then_inc(S["gates_full"][h], 1)
                elif kind == "lstm":
                    lstm_gates(h, job, g)
                elif kind == "norm":
                    wait(pe, "hidden", h, g, (LSTM_JOBS[-1], "low"))
                    for n in range(2):
                        for b in range(4 * n, 4 * n + 4):
                            to = bank[h][n][:, (b % 4) * P:(b % 4 + 1) * P]
                            mm(to, h_hi[h][:, b, :], ident16[:], start=True, stop=False)
                            last = mm(to, h_lo[h][:, b, :], ident16[:], start=False, stop=True)
                        last.then_inc(S["product_full"][h], 1)
                elif kind == "agg":
                    mix(h, job, g, (2, 3), lambda b: b2[:, b, :], ahatT[:],
                        lambda n: wait(pe, "normed", h, g, 0) if n == 0 else None)
                elif kind == "z1":
                    for c in range(2):
                        wait(pe, "evacuated", h, g, (("agg",), c))
                        for j in range(2):
                            mm(bank[h][2 * c + j][:], gw1_sb[:, j, :], buf1[h][:, c, :], start=True, stop=True
                               ).then_inc(S["product_full"][h], 1)

            def lstm_gates(h, job, g):
                _, p, k = job
                s, n_cols = p - SKIPS[0], GB * (P // p)
                prev = LSTM_JOBS[LSTM_JOBS.index(job) - 1]
                gates = gates_of(job)

                def part(gate, m, hi, lo, start, stop):
                    n = gates.index(gate)
                    to = bank[h][n][:, 0:n_cols].rearrange("p (b w) -> p b w", b=GB)
                    at = slice(GATE_AT[gate] * P, (GATE_AT[gate] + 1) * P)
                    mm(to, w_hi[:, s, m, at], hi, start=start, stop=False)
                    mm(to, w_hi[:, s, m, at], lo, start=False, stop=False)
                    return mm(to, w_lo[:, s, m, at], hi, start=False, stop=stop)

                xh, xl = window(h_hi[h], p, k), window(h_lo[h], p, k)
                if k == 0:
                    wait(pe, "hidden", h, g, (prev, "low"))
                    for gate in gates:
                        part(gate, 0, xh, xl, True, True).then_inc(S["gates_full"][h], 1)
                    return
                for gate in gates:
                    n = gates.index(gate)
                    if n < len(gates_of(prev)):
                        wait(pe, "gate_ready", h, g, (prev, gates_of(prev)[n]))
                    part(gate, 0, xh, xl, True, False)
                sh = s_hi[h][:, 0:n_cols].rearrange("p (b w) -> p b w", b=GB)
                sl = s_lo[h][:, 0:n_cols].rearrange("p (b w) -> p b w", b=GB)
                wait(pe, "hidden", h, g, (prev, "low"))
                for gate in gates:
                    part(gate, 1, sh, sl, False, True).then_inc(S["gates_full"][h], 1)

            with pe.Fori(0, GROUPS) as g:
                for h, job in order():
                    emit(h, job, g)

            with pe.Fori(0, CHUNKS // 2) as c:
                for h in range(2):
                    pe.wait_ge(z2_kept[h], c + 1)
                    pe.wait_ge(z2_bn[h], c + 1)
                    pe.wait_ge(r_ready[h], 2 * c + 2)
                    for j in range(2):
                        last = mm(bank[h][0][:], gw2_sb[:, j, :],
                                  z[:, bass.ds(2 * c + h, 1), j, :].rearrange("p o n -> p (o n)"),
                                  start=(j == 0), stop=(j == 1))
                    last.then_inc(z2_full[h], 1)

            with pe.Fori(0, GROUPS) as g:
                for h in range(2):
                    pe.wait_ge(y_res[h], 2 * g + 1)
                    for n in range(2):
                        pe.wait_ge(y_scaled[h], 2 * g + n + 1)
                        for b in range(4):
                            last = nc.tensor.transpose(bank[h][n][:, b * P:(b + 1) * P],
                                                       buf1[h][:, n, b * P:(b + 1) * P], ident[:])
                        last.then_inc(y_full[h], 1)

        @block.scalar
        def _(act):
            activation = nc.scalar.activation
            act.wait_ge(sem_setup, 6)

            def emit(h, job, g):
                kind = job[0]
                if kind in ("mix0", "agg"):
                    for n in range(2):
                        wait(act, "product_full", h, g, (job, n))
                        src = bank[h][n if kind == "mix0" else 2 + n]
                        activation(buf1[h][:, n, :], src[:], ACT.Copy).then_inc(S["evacuated"][h], 1)
                elif kind == "lin0":
                    for n in range(2):
                        wait(act, "biased", h, g, (job, n))
                        activation(buf2[h][:, n, :], buf2[h][:, n, :], ACT.Relu).then_inc(S["evacuated"][h], 1)
                elif kind == "mix1":
                    for n in range(2):
                        wait(act, "product_full", h, g, (job, n))
                        activation(buf2[h][:, n, :], bank[h][2 + n][:], ACT.Relu).then_inc(S["evacuated"][h], 1)
                elif kind == "lstm":
                    _, p, k = job
                    n_cols = BANK if p == 1 else GB * (P // p)
                    scale = 1.0 if p == 1 else 1.0 / (W_SCALE * H_SCALE)
                    for n, gate in enumerate(gates_of(job)):
                        wait(act, "gates_full", h, g, (job, gate))
                        if gate == "o" and job == ("lstm", 1, 1):
                            wait(act, "hidden", h, g, (("lstm", 1, 0), "h"))
                        activation(acts[gate][h][:, 0:n_cols], bank[h][lstm_bank(job, n)][:, 0:n_cols],
                                   ACT.Tanh if gate == "g" else ACT.Sigmoid,
                                   bias=lstm_bias[:, p - 1, GATE_AT[gate]:GATE_AT[gate] + 1],
                                   scale=scale).then_inc(S["gate_ready"][h], 1)
                    wait(act, "cell_part", h, g, (job, "cell"))
                    activation(tcell[h][:, 0:n_cols], cell[h][:, 0:n_cols], ACT.Tanh).then_inc(S["tanh_cell"][h], 1)
                elif kind == "z1":
                    for n in range(4):
                        c, j = n // 2, n % 2
                        wait(act, "product_full", h, g, (job, n))
                        activation(z[:, bass.ds(4 * g + 2 * h + c, 1), j, :].rearrange("p o n -> p (o n)"),
                                   bank[h][n][:], ACT.Identity, bias=v1_sb[:, 0, j:j + 1]
                                   ).then_inc(S["z_stored"][h], 1)

            with act.Fori(0, GROUPS) as g:
                for h, job in order():
                    emit(h, job, g)

            for h in range(2):
                wait_last(act, "z_stored", h, GROUPS)
            act.wait_ge(sem_bn1, 5)
            with act.Fori(0, CHUNKS // 2) as c:
                for h in range(2):
                    for j in range(2):
                        at = z[:, bass.ds(2 * c + h, 1), j, :].rearrange("p o n -> p (o n)")
                        activation(at, at, ACT.Relu, bias=small[:, 10 + j:11 + j], scale=small[:, 8 + j:9 + j]
                                   ).then_inc(r_ready[h], 1)

            act.wait_ge(sem_bn2, 5)
            with act.Fori(0, GROUPS) as g:
                for h in range(2):
                    act.wait_ge(y_full[h], 2 * g + 1)
                    for n in range(2):
                        activation(buf1[h][:, n, :],
                                   z[:, bass.ds(4 * g + 2 * h + n, 1), 0, :].rearrange("p o n -> p (o n)"),
                                   ACT.Identity, bias=small[:, 2:3], scale=small[:, 1:2]
                                   ).then_inc(y_scaled[h], 1)

        @block.vector
        def _(dve):
            ve = nc.vector
            dve.wait_ge(sem_loaded, 16 * LOADS)
            dve.wait_ge(sem_ident, 3)
            ve.tensor_copy(ident16[:], ident[:])
            ve.tensor_tensor(buf1[0][:, 0, 0:P], adj_sb[:], ident[:], ALU.mult)
            ve.tensor_tensor(buf1[0][:, 0, P:2 * P], adj_sb[:], adjT_sb[:], ALU.add)
            ve.tensor_tensor(adj_sb[:], adj_sb[:], ident[:], ALU.add).then_inc(sem_setup, 1)
            dve.wait_ge(sem_setup, 1)
            ve.tensor_tensor(buf1[0][:, 1, 0:P], buf1[0][:, 0, P:2 * P], buf1[0][:, 0, 0:P], ALU.subtract
                             ).then_inc(sem_degree, 1)
            dve.wait_ge(sem_degree, 1)
            ve.reduce_sum(small[:, 1:2], buf1[0][:, 1, 0:P], mybir.AxisListType.X).then_inc(sem_degree, 1)
            dve.wait_ge(sem_degree, 2)
            ve.tensor_scalar_add(small[:, 2:3], small[:, 1:2], 1.0).then_inc(sem_setup, 1)
            dve.wait_ge(sem_setup_pool, 1)
            ve.tensor_scalar(buf2[0][:, 0, 0:P], ident[:], small[:, 3:4], None, ALU.mult).then_inc(sem_setup, 1)
            ve.tensor_scalar(w_hi[:], w_stage, W_SCALE, None, ALU.mult).then_inc(sem_setup, 1)
            dve.wait_ge(sem_setup, 4)
            for s in range(3):
                for m in range(2):
                    ve.scalar_tensor_tensor(out=w_lo[:, s, m, :], in0=w_stage[:, s, m, :], scalar=W_SCALE,
                                            in1=w_hi[:, s, m, :], op0=ALU.mult, op1=ALU.subtract)
            ve.tensor_tensor(lstm_bias[:], lstm_bias[:], bhh_sb[:], ALU.add).then_inc(sem_setup, 1)
            dve.wait_ge(sem_setup_pe, 2)
            ve.tensor_copy(bias0[:], bank[0][0][:, 0:P])
            ve.tensor_scalar(ahatT[:], bank[0][1][:, 0:P], small[:, 3:4], None, ALU.mult).then_inc(sem_setup, 1)

            def over4(t):
                return t[:].unsqueeze(1).broadcast_to([P, 4, P])

            def emit(h, job, g):
                kind = job[0]
                b1 = buf1[h][:].rearrange("p a (b n) -> p (a b) n", n=P)
                b2 = buf2[h][:].rearrange("p a (b n) -> p (a b) n", n=P)
                if kind in ("lin0", "lin1"):
                    dst, base, bias = (b2, 2, bias0) if kind == "lin0" else (b1, 0, bias1)
                    if kind == "lin0":
                        dve.wait_ge(sem_kept[h], 16 * g + 1)
                    for n in range(2):
                        wait(dve, "product_full", h, g, (job, n))
                        ve.tensor_tensor(dst[:, 4 * n:4 * n + 4, :],
                                         bank[h][base + n][:].rearrange("p (b n) -> p b n", n=P),
                                         over4(bias), ALU.add).then_inc(S["biased"][h], 1)
                elif kind == "lstm":
                    lstm_state(h, job, g)
                elif kind == "norm":
                    for n in range(2):
                        wait(dve, "product_full", h, g, (job, n))
                        ve.scalar_tensor_tensor(out=buf1[h][:, n, :], in0=bank[h][n][:], scalar=1.0 / H_SCALE,
                                                in1=xin[h][:, 4 * n:4 * n + 4, :].rearrange("p b d -> p (b d)"),
                                                op0=ALU.mult, op1=ALU.add).then_inc(S["residual"][h], 1)
                    row_moments(h, buf1[h], lambda n: wait(dve, "residual", h, g, n), S["moments"][h],
                                lambda n: wait(dve, "moments", h, g, n))
                    wait(dve, "rstd", h, g, 0)
                    normalize(h, buf1[h], buf2[h], S["normed"][h])
                elif kind == "z1":
                    for n in range(4):
                        c, j = n // 2, n % 2
                        wait(dve, "z_stored", h, g, n)
                        last = ve.bn_stats(zbn[h][:, j, c, :], bank[h][n][:])
                    last.then_inc(S["z_stats"][h], 1)
                    wait(dve, "z_stats", h, g, "bn")
                    ve.tensor_copy(z_moments[:, :, bass.ds(4 * g + 2 * h, 2), :], zbn[h][:]
                                   ).then_inc(S["z_stats"][h], 1)

            def by_batch(t):
                return t[:].rearrange("p a (b n) -> p (a b) n", n=P)

            def row_moments(h, rows, wait_rows, moments, wait_moments):
                for b in range(GB):
                    if b % 4 == 0:
                        wait_rows(b // 4)
                    last = ve.bn_stats(bn[h][:, b, :], by_batch(rows)[:, b, :])
                last.then_inc(moments, 1)
                wait_moments(1)
                mean_e, m2_e, mean_o, m2_o = (bn[h][:, :, n] for n in (1, 2, 4, 5))
                apart, m2, mean = (comb[h][:, n, :] for n in range(3))
                ve.tensor_tensor(apart, mean_e, mean_o, ALU.subtract)
                ve.scalar_tensor_tensor(out=m2, in0=m2_e, scalar=P * EPS, in1=m2_o, op0=ALU.add, op1=ALU.add)
                ve.tensor_tensor(mean, mean_e, mean_o, ALU.add).then_inc(moments, 1)
                wait_moments(2)
                ve.tensor_scalar(mean, mean, 0.5, None, ALU.mult)
                ve.scalar_tensor_tensor(out=apart, in0=apart, scalar=0.25, in1=apart, op0=ALU.mult, op1=ALU.mult
                                        ).then_inc(moments, 1)
                wait_moments(3)
                ve.scalar_tensor_tensor(out=veps[h][:], in0=m2, scalar=1.0 / P, in1=apart, op0=ALU.mult,
                                        op1=ALU.add).then_inc(moments, 1)

            def normalize(h, rows, to, normed):
                for b in range(GB):
                    last = ve.tensor_scalar(by_batch(to)[:, b, :], by_batch(rows)[:, b, :], comb[h][:, 2, b:b + 1],
                                            rstd[h][:, b:b + 1], ALU.subtract, ALU.mult)
                last.then_inc(normed, 1)

            def lstm_state(h, job, g):
                _, p, k = job
                n_cols = BANK if p == 1 else GB * (P // p)
                i, gg, f, o = (acts[n][h][:, 0:n_cols] for n in ("i", "g", "f", "o"))
                c, tc = cell[h][:, 0:n_cols], tcell[h][:, 0:n_cols]
                part, hid = S["cell_part"][h], S["hidden"][h]
                wait(dve, "gate_ready", h, g, (job, "g"))
                if k == 0 or p == 1:
                    ve.tensor_tensor(c, i, gg, ALU.mult).then_inc(part, 1)
                else:
                    ve.tensor_tensor(i, i, gg, ALU.mult).then_inc(part, 1)
                    wait(dve, "gate_ready", h, g, (job, "f"))
                    ve.tensor_tensor(c, c, f, ALU.mult).then_inc(part, 1)
                    wait(dve, "cell_part", h, g, (job, "kept"))
                    ve.tensor_tensor(c, c, i, ALU.add).then_inc(part, 1)
                wait(dve, "tanh_cell", h, g, job)
                ve.scalar_tensor_tensor(out=f, in0=o, scalar=H_SCALE, in1=tc, op0=ALU.mult, op1=ALU.mult
                                        ).then_inc(hid, 1)
                if p == 1:
                    hi = h_hi[h][:, 4 * k:4 * k + 4, :].rearrange("p b t -> p (b t)")
                    lo = h_lo[h][:, 4 * k:4 * k + 4, :].rearrange("p b t -> p (b t)")
                    src = f
                elif k < p - 1:
                    hi, lo, src = s_hi[h][:, 0:n_cols], s_lo[h][:, 0:n_cols], f
                else:
                    hi, lo = window(h_hi[h], p, k), window(h_lo[h], p, k)
                    src = f.rearrange("p (b w) -> p b w", b=GB)
                wait(dve, "hidden", h, g, (job, "h"))
                ve.tensor_copy(hi, src).then_inc(hid, 1)
                wait(dve, "hidden", h, g, (job, "high"))
                ve.tensor_tensor(lo, src, hi, ALU.subtract).then_inc(hid, 1)

            with dve.Fori(0, GROUPS) as g:
                for h, job in order():
                    emit(h, job, g)

            for h in range(2):
                wait_last(dve, "z_stats", h, GROUPS)
            for j in range(2):
                last = ve.bn_aggr(mv[:, j, :], z_moments[:, j, :, :].rearrange("p c s -> p (c s)"))
            last.then_inc(sem_bn1, 1)
            dve.wait_ge(sem_bn1, 1)
            ve.tensor_tensor(small[:, 14:16], mv[:, 0:2, 0], v1_sb[:, 0, :], ALU.add)
            ve.tensor_scalar_add(small[:, 4:6], mv[:, 0:2, 1], EPS).then_inc(sem_bn1, 1)
            dve.wait_ge(sem_bn1_pow, 1)
            ve.tensor_tensor(small[:, 8:10], small[:, 6:8], v1_sb[:, 1, :], ALU.mult).then_inc(sem_bn1, 1)
            dve.wait_ge(sem_bn1, 3)
            ve.tensor_tensor(small[:, 14:16], small[:, 14:16], small[:, 8:10], ALU.mult).then_inc(sem_bn1, 1)
            dve.wait_ge(sem_bn1, 4)
            ve.tensor_tensor(small[:, 10:12], v1_sb[:, 2, :], small[:, 14:16], ALU.subtract).then_inc(sem_bn1, 1)

            with dve.Fori(0, CHUNKS // 2) as c:
                for h in range(2):
                    dve.wait_ge(z2_full[h], c + 1)
                    ve.bn_stats(zbn[h][:, 0, 0, :], bank[h][0][:]).then_inc(z2_bn[h], 1)
                    ve.tensor_scalar(z[:, bass.ds(2 * c + h, 1), 0, :].rearrange("p o n -> p (o n)"),
                                     bank[h][0][:], v2_sb[:, 0:1], None, ALU.add).then_inc(z2_kept[h], 1)
                    dve.wait_ge(z2_bn[h], c + 2)
                    ve.tensor_copy(z_moments[:, 0, bass.ds(2 * c + h, 1), :].rearrange("p o s -> p (o s)"),
                                   zbn[h][:, 0, 0, :]).then_inc(z2_moments[h], 1)

            for h in range(2):
                dve.wait_ge(z2_moments[h], CHUNKS // 2)
                dve.wait_ge(z2_kept[h], CHUNKS // 2 + 1)
            ve.bn_aggr(mv[:, 0, :], z_moments[:, 0, :, :].rearrange("p c s -> p (c s)")).then_inc(sem_bn2, 1)
            dve.wait_ge(sem_bn2, 1)
            ve.tensor_tensor(small[:, 14:15], mv[:, 0, 0:1], v2_sb[:, 0:1], ALU.add)
            ve.tensor_scalar_add(small[:, 12:13], mv[:, 0, 1:2], EPS).then_inc(sem_bn2, 1)
            dve.wait_ge(sem_bn2_pow, 1)
            ve.tensor_tensor(small[:, 1:2], small[:, 13:14], v2_sb[:, 1:2], ALU.mult).then_inc(sem_bn2, 1)
            dve.wait_ge(sem_bn2, 3)
            ve.tensor_tensor(small[:, 15:16], small[:, 14:15], small[:, 1:2], ALU.mult).then_inc(sem_bn2, 1)
            dve.wait_ge(sem_bn2, 4)
            ve.tensor_tensor(small[:, 2:3], v2_sb[:, 2:3], small[:, 15:16], ALU.subtract).then_inc(sem_bn2, 1)

            with dve.Fori(0, GROUPS) as g:
                for h in range(2):
                    dve.wait_ge(x1_back[h], 16 * g + 16)
                    dve.wait_ge(y_out[h], 16 * g + 1)
                    for n in range(2):
                        dve.wait_ge(y_full[h], 2 * g + n + 2)
                        ve.tensor_tensor(buf2[h][:, n, :], bank[h][n][:],
                                         xin[h][:, 4 * n:4 * n + 4, :].rearrange("p b d -> p (b d)"), ALU.add
                                         ).then_inc(y_res[h], 1)
                    row_moments(h, buf2[h], lambda n: dve.wait_ge(y_res[h], 2 * g + n + 2), y_mom[h],
                                lambda n: dve.wait_ge(y_mom[h], 4 * g + n))
                    dve.wait_ge(y_rstd[h], g + 1)
                    normalize(h, buf2[h], buf2[h], y_norm[h])
        return nc


INPUTS = ("x", "adj", "adjT", "w0", "b0_rep", "w1", "b1_rep", "wih1", "b_ih", "b_hh", "wr", "gw1", "gw2",
          "vec1", "vec2")


def kernel(**inputs):
    import concourse.bacc as bacc
    from concourse.bass_utils import run_bass_kernel_spmd

    a = {k: np.asarray(v) for k, v in inputs.items()}
    x = a["x"]
    nb = x.shape[0]
    wih, whh = a["L0_gnn_Wih"], a["L0_gnn_Whh"]
    laid = {
        "x": x.reshape(nb // GB, GB, P, P).transpose(0, 2, 1, 3).reshape(nb // GB, P, GB * P),
        "adj": a["adj"],
        "adjT": a["adj"].T,
        "w0": a["L0_gnn_Wg0"],
        "b0_rep": np.broadcast_to(a["L0_gnn_bg0"][None, :], (P, P)),
        "w1": a["L0_gnn_Wg1"],
        "b1_rep": np.broadcast_to(a["L0_gnn_bg1"][None, :], (P, P)),
        "wih1": np.stack([wih[0, GATE_AT[n] * P:(GATE_AT[n] + 1) * P].T for n in GATES_FIRST], axis=1),
        "b_ih": a["L0_gnn_bih"].reshape(4, 4, P).transpose(2, 0, 1),
        "b_hh": a["L0_gnn_bhh"].reshape(4, 4, P).transpose(2, 0, 1),
        "wr": np.stack([wih[1:], whh[1:]], axis=1).transpose(3, 0, 1, 2),
        "gw1": a["L1_gnn_W1"].reshape(2, P, P).transpose(2, 0, 1),
        "gw2": a["L1_gnn_W2"].reshape(P, 2, P).transpose(2, 1, 0),
        "vec1": np.stack([a[f"L1_gnn_{n}"].reshape(2, P).T for n in ("b1", "g1", "be1")], axis=1),
        "vec2": np.stack([a[f"L1_gnn_{n}"] for n in ("b2", "g2", "be2")], axis=1),
    }
    nc = bacc.Bacc("TRN2", target_bir_lowering=False, num_devices=1)
    arrays, args = {}, []
    for name in INPUTS:
        arrays[f"in_{name}"] = np.ascontiguousarray(laid[name])
        args.append(nc.dram_tensor(f"in_{name}", arrays[f"in_{name}"].shape, F32, kind="ExternalInput").ap())
    out = nc.dram_tensor("out", (nb // GB, P, GB * P), F32, kind="ExternalOutput").ap()
    gnn_lstm_kernel(nc, *args, out)
    result = run_bass_kernel_spmd(nc, [arrays], core_ids=[0]).results[0]["out"]
    return result.reshape(nb // GB, P, GB, P).transpose(0, 2, 1, 3).reshape(nb, P, P)
```

```python
from contextlib import ExitStack

import numpy as np

import concourse.bass as bass
from concourse import mybir

F32 = mybir.dt.float32
F16 = mybir.dt.float16
ALU = mybir.AluOpType
ACT = mybir.ActivationFunctionType

P = 128
BANK = 512
EPS = 1e-5
GB = 8
SKIPS = (2, 3, 4)
W_SCALE = 2.0 ** 6
H_SCALE = 2.0 ** 14
GATES_FIRST = ("i", "g", "o")
GATES_NEXT = ("i", "g", "f", "o")
GATE_AT = {"i": 0, "f": 1, "g": 2, "o": 3}

LSTM_JOBS = [("lstm", 1, c) for c in range(2)] + [("lstm", p, k) for p in SKIPS for k in range(p)]


def gates_of(job):
    return GATES_FIRST if job[1] == 1 or job[2] == 0 else GATES_NEXT


def columns_of(job):
    return BANK if job[1] == 1 else GB * (P // job[1])


def matmul_us(columns, passes):
    return passes * (columns / 2.4 + 2.5) / 1e3


MIX_US = 2 * matmul_us(2 * P, 1)
WIDE_US = 2 * matmul_us(2 * BANK, 1)


def vector_us(columns, rate=1):
    return (77 + columns / rate) / 960 - 0.01


def scalar_us(columns, pointers):
    return (51 + 93 * pointers + columns / 1.2) / 1e3


def front_stage():
    ops, bank_free = [], None
    for stage, parts, before in (("mix0", 4, None), ("lin0", 1, "mix0"), ("lin1", 4, "lin0"), ("mix1", 4, "lin1")):
        for n in range(2):
            after = [(before, "out", n)] if before else []
            after += [bank_free] if bank_free else []
            for i in range(parts):
                ops.append(("PE", (stage, "product", n, i), MIX_US if parts == 4 else WIDE_US,
                            after if i == 0 else []))
            after = [(stage, "product", n, parts - 1)]
            if stage == "lin0":
                ops.append(("DVE", (stage, "biased", n), vector_us(BANK), after))
                after = [(stage, "biased", n)]
            ops.append(("DVE" if stage == "lin1" else "ACT", (stage, "out", n), scalar_us(BANK, 0), after))
            bank_free = (stage, "biased" if stage == "lin0" else "out", n)
    return ops


BANK_OF = {"i": 0, "g": 1, "f": 2, "o": 0}


def bank_of(job, gate):
    return 2 if gate == "o" and gates_of(job) == GATES_FIRST else BANK_OF[gate]


def bank_reader(job, gate):
    return [n for n in gates_of(job) if bank_of(job, n) == BANK_OF[gate]][-1]


def lstm_stage():
    ops, prev = [], None
    for job in LSTM_JOBS:
        n = columns_of(job)
        gates = gates_of(job)
        if job[1] == 1:
            for gate in gates:
                after = [("mix1", "out", job[2])] if gate == "i" else []
                after += [(prev, "act", gate)] if job[2] == 1 else []
                ops.append(("PE", (job, "gate", gate), WIDE_US, after))
        elif job[2] == 0:
            for gate in gates:
                ops.append(("PE", (job, "gate", gate), matmul_us(n, 3), [(prev, "low")]))
        else:
            for gate in "igf":
                ops.append(("PE", (job, "input", gate), matmul_us(n, 3), [(prev, "act", bank_reader(prev, gate))]))
            for gate in "ig":
                ops.append(("PE", (job, "high", gate), matmul_us(n, 2), [(prev, "high")]))
            for gate in "ig":
                ops.append(("PE", (job, "gate", gate), matmul_us(n, 1), [(prev, "low")]))
            ops.append(("PE", (job, "gate", "f"), matmul_us(n, 3), []))
            ops.append(("PE", (job, "input", "o"), matmul_us(n, 3), [(job, "act", "i")]))
            ops.append(("PE", (job, "gate", "o"), matmul_us(n, 3), []))
        for gate in gates:
            ops.append(("ACT", (job, "act", gate), scalar_us(n, 1), [(job, "gate", gate)]))
            if gate == "g":
                ops.append(("DVE", (job, "new"), vector_us(n), [(job, "act", "g")]))
            if gate == "f":
                ops.append(("DVE", (job, "kept"), vector_us(n), [(job, "act", "f")]))
                ops.append(("DVE", (job, "cell"), vector_us(n), [(job, "kept")]))
        ops.append(("ACT", (job, "tanh"), scalar_us(n, 0) + 0.04, [(job, "cell" if "f" in gates else "new")]))
        ops.append(("DVE", (job, "hidden"), vector_us(n), [(job, "tanh")]))
        ops.append(("DVE", (job, "high"), vector_us(n, 2), [(job, "hidden")]))
        ops.append(("DVE", (job, "low"), vector_us(n), [(job, "high")]))
        prev = job
    return ops


def back_stage():
    ops = []
    for n in range(2):
        for i in range(2):
            after = [("back", "residual", 0)] if n else [(LSTM_JOBS[-1], "low")]
            ops.append(("PE", ("back", "tokens", n, i), matmul_us(P, 4), after if i == 0 else []))
        ops.append(("DVE", ("back", "residual", n), vector_us(BANK), [("back", "tokens", n, 1)]))
    for n in range(2):
        ops.append(("DVE", ("back", "stats", n), 0.81, [("back", "residual", n)]))
    for n in range(3):
        ops.append(("DVE", ("back", "moments", n), 0.25,
                    [("back", "moments", n - 1) if n else ("back", "stats", 1)]))
    ops.append(("POOL", ("back", "rstd"), 0.3, [("back", "moments", 2)]))
    for n in range(2):
        ops.append(("DVE", ("back", "normed", n), 1.02, [("back", "rstd")]))
    for n in range(2):
        for i in range(4):
            after = [("back", "normed", n)] + ([("back", "mixed", 0)] if n else [])
            ops.append(("PE", ("back", "mix", n, i), MIX_US, after if i == 0 else []))
        ops.append(("ACT", ("back", "mixed", n), scalar_us(BANK, 0), [("back", "mix", n, 3)]))
    for n in range(4):
        ops.append(("PE", ("back", "z", n), WIDE_US, [("back", "z_stats", n - 1) if n else ("back", "mixed", 1)]))
        ops.append(("ACT", ("back", "z_stored", n), scalar_us(BANK, 1), [("back", "z", n)]))
        ops.append(("DVE", ("back", "z_stats", n), vector_us(BANK), [("back", "z_stored", n)]))
    return ops


def signal_of(op):
    what = op[1]
    if isinstance(op[0], tuple):
        return {"gate": "gates_full", "act": "gate_ready", "tanh": "tanh_cell", "new": "cell_part",
                "kept": "cell_part", "cell": "cell_part", "hidden": "hidden_part", "high": "hidden_part",
                "low": "hidden_part", "input": None}[what] if not (what == "high" and len(op) == 3) else None
    if op[0] == "back":
        return {"tokens": "back_product", "mix": "back_product", "z": "back_product", "rstd": "rstd",
                "residual": "residual", "stats": "moments", "moments": "moments", "normed": "normed",
                "mixed": "mixed", "z_stored": "z_stored", "z_stats": "z_stats"}[what]
    if what == "product":
        return "front_product"
    return "front_biased" if what == "biased" or op[0] == "lin1" else "front_out"


def count_signals():
    total, at = {}, {}
    for _, op, _, _ in front_stage() + lstm_stage() + back_stage():
        name = signal_of(op)
        if name:
            total[name] = total.get(name, 0) + 1
            at[op] = total[name]
    return total, at


EARLIER = {
    ("mix0", "product", 0, 0): (1, ("mix1", "out", 1)),
    ("mix1", "out", 0): (1, (LSTM_JOBS[0], "gate", "o")),
    ("mix1", "out", 1): (1, (LSTM_JOBS[1], "gate", "o")),
    (LSTM_JOBS[0], "gate", "i"): (2, (LSTM_JOBS[-1], "act", "o")),
    (LSTM_JOBS[0], "act", "o"): (2, (LSTM_JOBS[-1], "hidden")),
    (LSTM_JOBS[0], "high"): (2, ("back", "tokens", 1, 1)),
    ("back", "tokens", 0, 0): (1, ("back", "z_stats", 3)),
}


def plan_order(halves):
    streams = {"front": (front_stage(), range(halves)), "even": (lstm_stage(), range(0, halves, 2)),
               "odd": (lstm_stage(), range(1, halves, 2)), "back": (back_stage(), range(halves))}
    rank = {"front": 0, "back": 1, "even": 2, "odd": 2}
    engines = ("PE", "ACT", "DVE", "POOL")
    queue = {(s, e): [(q, *o[1:]) for q in qs for o in ops if o[0] == e]
             for s, (ops, qs) in streams.items() for e in engines}
    at = dict.fromkeys(queue, 0)
    done, free, order = {}, dict.fromkeys(engines, 0.0), {e: [] for e in engines}
    while True:
        best = None
        for e in engines:
            for s in streams:
                if at[s, e] >= len(queue[s, e]):
                    continue
                q, op, us, after = queue[s, e][at[s, e]]
                needs = [(q, x) for x in after]
                if op in EARLIER and q >= EARLIER[op][0]:
                    needs.append((q - EARLIER[op][0], EARLIER[op][1]))
                if any(x not in done for x in needs):
                    continue
                start = max([free[e]] + [done[x] + 0.13 for x in needs])
                key = (round(start, 6), rank[s], q)
                if best is None or key < best[0]:
                    best = (key, e, s, q, op, start, us)
        if best is None:
            return order
        _, e, s, q, op, start, us = best
        done[q, op] = free[e] = start + us
        at[s, e] += 1
        order[e].append((start, q, op))


def cut_order(halves):
    order = plan_order(halves)
    cuts = [t for t, q, op in order["PE"] if op == ("mix0", "product", 0, 0) and q % 2 == 0]
    chunks = {e: [[(q - 2 * k, op) for t, q, op in ops
                   if (k == 0 or t >= cuts[k]) and (k + 1 == len(cuts) or t < cuts[k + 1])]
                  for k in range(len(cuts))] for e, ops in order.items()}
    runs = [(k0, k1) for k0 in range(1, len(cuts)) for k1 in range(k0 + 1, len(cuts))
            if all(c[k] == c[k0] for c in chunks.values() for k in range(k0, k1))
            and all(q + 2 * k0 >= EARLIER.get(op, (0,))[0] for c in chunks.values() for q, op in c[k0])]
    return chunks, max(runs, key=lambda r: r[1] - r[0])


def gnn_lstm_kernel(nc, x, adj, adjT, w0, b0_rep, w1, b1_rep, wih1, b_ih, b_hh, wr, gw1, gw2, vec1, vec2, out):
    NB = x.shape[0] * GB
    HALVES = x.shape[0]
    GROUPS = HALVES // 2
    HW = GB * P
    CHUNKS = HALVES * 2
    PER, AT = count_signals()
    CHUNK_OF, (LOOP_FROM, LOOP_TO) = cut_order(HALVES)

    x1_dram = nc.dram_tensor("x1_kept", [HALVES, P, HW], F32, kind="Internal").ap()

    with ExitStack() as ctx:
        def sb(name, shape, dt=F32):
            return ctx.enter_context(nc.sbuf_tensor(name, shape, dt))

        def sem(name):
            return ctx.enter_context(nc.semaphore(name))

        adj_sb = sb("adj_sb", [P, P])
        adjT_sb = sb("adjT_sb", [P, P])
        ahatT = sb("ahatT", [P, P])
        ident = sb("ident", [P, P])
        ident16 = sb("ident16", [P, P], F16)
        w0_sb = sb("w0_sb", [P, P])
        w1_sb = sb("w1_sb", [P, P])
        bias0 = sb("bias0", [P, P])
        bias1 = sb("bias1", [P, P])
        wih1_sb = sb("wih1_sb", [P, 3, P])
        w_hi = sb("w_hi", [P, len(SKIPS), 2, 4 * P], F16)
        w_lo = sb("w_lo", [P, len(SKIPS), 2, 4 * P], F16)
        lstm_bias = sb("lstm_bias", [P, 4, 4])
        bhh_sb = sb("bhh_sb", [P, 4, 4])
        gw1_sb = sb("gw1_sb", [P, 2, P])
        gw2_sb = sb("gw2_sb", [P, 2, P])
        v1_sb = sb("v1_sb", [P, 3, 2])
        v2_sb = sb("v2_sb", [P, 3])
        small = sb("small", [P, 16])
        neg_half = sb("neg_half", [P, GB])

        z = sb("z", [P, CHUNKS, 2, BANK])
        z_moments = sb("z_moments", [P, 2, CHUNKS, 6])

        x_front = sb("x_front", [P, 2, BANK])
        mixed = sb("mixed", [P, 2, BANK])
        h0T = sb("h0T", [P, 2, BANK])
        h1T = sb("h1T", [P, 2, BANK])

        def two(name, shape, dt=F32):
            return [sb(f"{name}{h}", shape, dt) for h in range(2)]

        h_hi = two("h_hi", [P, GB, P], F16)
        h_lo = two("h_lo", [P, GB, P], F16)
        s_hi = two("s_hi", [P, BANK], F16)
        s_lo = two("s_lo", [P, BANK], F16)
        acts = {n: two(f"gate_{n}", [P, BANK]) for n in "igfo"}
        cell = two("cell", [P, BANK])

        rows_sb = sb("rows_sb", [P, 2, BANK])
        normed_sb = sb("normed_sb", [P, 2, BANK])
        rows = rows_sb
        normed = [normed_sb, h1T]
        x1_again = [rows_sb, x_front]
        scaled = [mixed, h0T]
        bn = two("bn", [P, GB, 6])
        comb = two("comb", [P, 3, GB])
        veps = two("veps", [P, GB])
        rstd = two("rstd", [P, GB])
        mv = sb("mv", [P, 2, 2])
        w_stage = z[:, 0:len(SKIPS), :, :]

        gate_bank = [[ctx.enter_context(nc.psum_tensor(f"gate_bank{h}{n}", [P, BANK], F32)) for n in range(3)]
                     for h in range(2)]
        front_bank = ctx.enter_context(nc.psum_tensor("front_bank", [P, BANK], F32))
        back_bank = ctx.enter_context(nc.psum_tensor("back_bank", [P, BANK], F32))

        sem_first = sem("first_weights_loaded")
        sem_loaded = sem("weights_loaded")
        sem_wr = sem("recurrent_weights_loaded")
        sem_ident = sem("ident_ready")
        sem_setup = sem("setup_step")
        sem_degree = sem("degree_step")
        sem_setup_pe = sem("setup_product")
        sem_setup_pool = sem("setup_pow")
        sem_ahat = sem("ahat_ready")
        sem_split = sem("weights_split")
        sem_x = sem("x_front_loaded")
        sem_xb = sem("x_back_loaded")
        sem_kept = sem("x1_kept")
        lstm_signals = ("gates_full", "gate_ready", "tanh_cell", "cell_part", "hidden_part")
        S = {name: [sem(f"{name}{h}") for h in range(2)] if name in lstm_signals else sem(name) for name in PER}
        sem_bn1 = sem("bn1_step")
        sem_bn1_pow = sem("bn1_pow")
        r_ready = [sem(f"r_ready{h}") for h in range(2)]
        z2_full = [sem(f"z2_full{h}") for h in range(2)]
        z2_bn = [sem(f"z2_bn{h}") for h in range(2)]
        z2_kept = [sem(f"z2_kept{h}") for h in range(2)]
        sem_bn2 = sem("bn2_step")
        sem_bn2_pow = sem("bn2_pow")
        y_scaled = [sem(f"y_scaled{h}") for h in range(2)]
        z2_moments = [sem(f"z2_moments{h}") for h in range(2)]
        x1_back = [sem(f"x1_back{h}") for h in range(2)]
        y_full = [sem(f"y_full{h}") for h in range(2)]
        y_res = [sem(f"y_res{h}") for h in range(2)]
        y_mom = [sem(f"y_moments{h}") for h in range(2)]
        y_rstd = [sem(f"y_rstd{h}") for h in range(2)]
        y_norm = [sem(f"y_normed{h}") for h in range(2)]
        y_out = [sem(f"y_stored{h}") for h in range(2)]

        def signal(ins, op, h):
            name = signal_of(op)
            ins.then_inc(S[name][h] if name in lstm_signals else S[name], 1)

        def wait(eng, op, g, h):
            name = signal_of(op)
            if name in lstm_signals:
                eng.wait_ge(S[name][h], g * PER[name] + AT[op])
            else:
                eng.wait_ge(S[name], g * (2 * PER[name]) + (h * PER[name] + AT[op]))

        def wait_earlier(eng, op, g, h, by):
            h_then = (h - by) % 2
            g_then = g + (h - by) // 2 if (h - by) // 2 else g
            if not (isinstance(g_then, int) and g_then < 0):
                wait(eng, op, g_then, h_then)

        def loads(g, h, extra=0):
            return g * 32 + (16 * h + 16 + extra)

        def run(eng, engine, emit):
            def chunk(k, at):
                for q, op in CHUNK_OF[engine][at]:
                    emit(op, k + q // 2 if q // 2 else k, q % 2)
            for k in range(LOOP_FROM):
                chunk(k, k)
            with eng.Fori(LOOP_FROM, LOOP_TO) as k:
                chunk(k, LOOP_FROM)
            for k in range(LOOP_TO, len(CHUNK_OF[engine])):
                chunk(k, k)

        free_at_start = [z2_bn, z2_kept, y_full, y_res, y_out]
        FIRST_LOADS, LOADS = 5, 8
        block = ctx.enter_context(nc.Block())

        def flat(t):
            return t.rearrange("p a n -> p (a n)")

        def half_of(dram, g, h):
            if isinstance(g, int):
                return dram[2 * g + h]
            return dram[bass.ds(2 * g + h, 1)].rearrange("o p n -> p (o n)")

        @block.sync
        def _(sp):
            sp.dma_start(flat(x_front[:]), x[0]).then_inc(sem_x, 16)
            for dst, src in ((adjT_sb[:], adjT), (adj_sb[:], adj), (w0_sb[:], w0), (bias0[:], b0_rep),
                             (w1_sb[:], w1)):
                sp.dma_start(dst, src).then_inc(sem_first, 16)
            for dst, src in ((bias1[:], b1_rep), (lstm_bias[:], b_ih), (bhh_sb[:], b_hh), (wih1_sb[:], wih1),
                             (gw1_sb[:], gw1), (gw2_sb[:], gw2), (v1_sb[:], vec1), (v2_sb[:], vec2)):
                sp.dma_start(dst, src).then_inc(sem_loaded, 16)
            sp.dma_start(w_stage, wr).then_inc(sem_wr, 16)
            sp.dma_start(flat(rows[:]), x[0]).then_inc(sem_xb, 16)

            def next_front(g, h):
                wait(sp, ("mix0", "product", 1, 3), g, h)
                g_next, h_next = (g, 1) if h == 0 else (g + 1, 0)
                sp.dma_start(flat(x_front[:]), half_of(x, g_next, h_next)).then_inc(sem_x, 16)

            def back(g, h, more=True):
                wait(sp, ("back", "normed", 1), g, h)
                sp.dma_start(half_of(x1_dram, g, h), flat(normed[0][:])).then_inc(sem_kept, 16)
                if more:
                    wait(sp, ("back", "z", 3), g, h)
                    g_next, h_next = (g, 1) if h == 0 else (g + 1, 0)
                    sp.dma_start(flat(rows[:]), half_of(x, g_next, h_next)).then_inc(sem_xb, 16)

            for q in range(4):
                next_front(q // 2, q % 2)
            back(0, 0)
            with sp.Fori(2, GROUPS - 1) as g:
                next_front(g, 0)
                back(g - 2, 1)
                next_front(g, 1)
                back(g - 1, 0)
            next_front(GROUPS - 1, 0)
            back(GROUPS - 3, 1)
            for q in range(HALVES - 4, HALVES):
                back(q // 2, q % 2, q + 1 < HALVES)

            sp.wait_ge(sem_kept, 16 * HALVES)
            wait(sp, ("back", "z", 3), GROUPS - 1, 1)
            for h in range(2):
                sp.dma_start(flat(x1_again[h][:]), x1_dram[h]).then_inc(x1_back[h], 16)

            def store(h, g):
                sp.wait_ge(y_norm[h], g + 1)
                sp.dma_start(half_of(out, g, h), flat(normed[h][:])).then_inc(y_out[h], 16)

            with sp.Fori(0, GROUPS - 1) as g:
                for h in range(2):
                    sp.wait_ge(y_res[h], 2 * g + 3)
                    sp.dma_start(flat(x1_again[h][:]), half_of(x1_dram, g + 1, h)).then_inc(x1_back[h], 16)
                    store(h, g)
            for h in range(2):
                store(h, GROUPS - 1)
            for h in range(2):
                sp.wait_ge(y_out[h], 16 * GROUPS + 1)

        @block.gpsimd
        def _(pool):
            for pair in free_at_start:
                for s in pair:
                    pool.sem_inc(s, 1)
            nc.gpsimd.memset(ident[:], 0.0).then_inc(sem_ident, 1)
            nc.gpsimd.memset(neg_half[:], -0.5).then_inc(sem_ident, 1)
            pool.wait_ge(sem_ident, 2)
            nc.gpsimd.affine_select(out=ident[:], in_=ident[:], compare_op=ALU.not_equal, fill=1.0, base=0,
                                    pattern=[[-1, P]], channel_multiplier=1).then_inc(sem_ident, 1)
            pool.wait_ge(sem_degree, 4)
            nc.gpsimd.tensor_tensor(small[:, 3:4], small[:, 2:3], neg_half[:, 0:1], ALU.pow).then_inc(sem_setup_pool, 1)

            def emit(op, g, h):
                wait(pool, ("back", "moments", 2), g, h)
                signal(nc.gpsimd.tensor_tensor(rstd[0][:], veps[0][:], neg_half[:], ALU.pow), op, h)

            run(pool, "POOL", emit)
            pool.wait_ge(sem_bn1, 2)
            nc.gpsimd.tensor_tensor(small[:, 6:8], small[:, 4:6], neg_half[:, 0:2], ALU.pow).then_inc(sem_bn1_pow, 1)
            pool.wait_ge(sem_bn2, 2)
            nc.gpsimd.tensor_tensor(small[:, 13:14], small[:, 12:13], neg_half[:, 0:1], ALU.pow).then_inc(sem_bn2_pow, 1)
            with pool.Fori(0, GROUPS) as g:
                for h in range(2):
                    pool.wait_ge(y_mom[h], 4 * g + 4)
                    nc.gpsimd.tensor_tensor(rstd[h][:], veps[h][:], neg_half[:], ALU.pow).then_inc(y_rstd[h], 1)

        def window(t, p, k):
            nw = P // p
            return t[:, :, k:k + p * (nw - 1) + 1:p]

        @block.tensor
        def _(pe):
            mm = nc.tensor.matmul
            pe.wait_ge(sem_first, 16 * FIRST_LOADS)
            mm(back_bank[:, 0:P], bias0[:], adjT_sb[:], start=True, stop=True).then_inc(sem_setup_pe, 1)

            def emit(op, g, h):
                if isinstance(op[0], tuple):
                    lstm_product(op, g, h)
                elif op[0] == "back":
                    back_product(op, g, h)
                else:
                    front_product(op, g, h)
                if op == ("mix1", "product", 1, 3) and isinstance(g, int) and (g, h) == (0, 0):
                    pe.wait_ge(sem_setup, 2)
                    mm(back_bank[:, 0:P], adj_sb[:], normed_sb[:, 1, P:2 * P], start=True, stop=True
                       ).then_inc(sem_setup_pe, 1)

            def front_product(op, g, h):
                stage, _, n, i = op
                b = 4 * n + i
                cols = front_bank[:, i * P:(i + 1) * P]
                if stage == "mix0":
                    if (n, i) == (0, 0):
                        pe.wait_ge(sem_x, loads(g, h))
                        wait_earlier(pe, ("mix1", "out", 1), g, h, 1)
                    if (n, i) == (1, 0):
                        wait(pe, ("mix0", "out", 0), g, h)
                    ins = mm(cols, x_front[:, n, i * P:(i + 1) * P], adjT_sb[:], start=True, stop=True)
                elif stage == "lin0":
                    wait(pe, ("mix0", "out", 1), g, h)
                    if n == 1:
                        wait(pe, ("lin0", "biased", 0), g, h)
                    ins = mm(front_bank[:], w0_sb[:], mixed[:, n, :], start=True, stop=True)
                elif stage == "lin1":
                    if i == 0:
                        wait(pe, ("lin0", "out", n), g, h)
                        wait(pe, ("lin0", "biased", 1) if n == 0 else ("lin1", "out", 0), g, h)
                    ins = mm(cols, flat(h0T[:])[:, b * P:(b + 1) * P], w1_sb[:], start=True, stop=True)
                else:
                    if i == 0:
                        wait(pe, ("lin1", "out", 1), g, h)
                        if n == 1:
                            wait(pe, ("mix1", "out", 0), g, h)
                    ins = mm(cols, flat(mixed[:])[:, b * P:(b + 1) * P], adjT_sb[:], start=True, stop=True)
                signal(ins, op, h)

            def back_product(op, g, h):
                _, what, n = op[0:3]
                if what == "tokens":
                    if (n, op[3]) == (0, 0):
                        wait(pe, (LSTM_JOBS[-1], "low"), g, h)
                        wait_earlier(pe, ("back", "z_stats", 3), g, h, 1)
                    if (n, op[3]) == (1, 0):
                        wait(pe, ("back", "residual", 0), g, h)
                    for b in (2 * op[3], 2 * op[3] + 1):
                        to = back_bank[:, b * P:(b + 1) * P]
                        mm(to, h_hi[h][:, 4 * n + b, :], ident16[:], start=True, stop=False)
                        ins = mm(to, h_lo[h][:, 4 * n + b, :], ident16[:], start=False, stop=True)
                elif what == "mix":
                    i = op[3]
                    if i == 0:
                        wait(pe, ("back", "normed", n), g, h)
                        if n == 1:
                            wait(pe, ("back", "mixed", 0), g, h)
                    if i == 0 and n == 0:
                        pe.wait_ge(sem_ahat, 1)
                    ins = mm(back_bank[:, i * P:(i + 1) * P], normed[0][:, n, i * P:(i + 1) * P], ahatT[:],
                             start=True, stop=True)
                else:
                    wait(pe, ("back", "z_stats", n - 1) if n else ("back", "mixed", 1), g, h)
                    ins = mm(back_bank[:], gw1_sb[:, n % 2, :], rows[:, n // 2, :], start=True, stop=True)
                signal(ins, op, h)

            def lstm_product(op, g, h):
                job, what, gate = op
                _, p, k = job
                to = gate_bank[h][bank_of(job, gate)]
                if p == 1:
                    if gate == "i":
                        wait(pe, ("mix1", "out", k), g, h)
                        if k == 0:
                            pe.wait_ge(sem_loaded, 16 * LOADS)
                            wait_earlier(pe, (LSTM_JOBS[-1], "act", "o"), g, h, 2)
                    if k == 1:
                        wait(pe, (LSTM_JOBS[0], "act", gate), g, h)
                    signal(mm(to[:], wih1_sb[:, GATES_FIRST.index(gate), :], h1T[:, k, :], start=True, stop=True),
                           op, h)
                    return
                s, n = p - SKIPS[0], columns_of(job)
                to = to[:, 0:n].rearrange("p (b w) -> p b w", b=GB)
                rows_at = slice(GATE_AT[gate] * P, (GATE_AT[gate] + 1) * P)
                w_in = w_hi[:, s, 0, rows_at], w_lo[:, s, 0, rows_at]
                w_rec = w_hi[:, s, 1, rows_at], w_lo[:, s, 1, rows_at]
                state = [t[h][:, 0:n].rearrange("p (b w) -> p b w", b=GB) for t in (s_hi, s_lo)]
                seen = [window(t[h], p, k) for t in (h_hi, h_lo)]
                prev = LSTM_JOBS[LSTM_JOBS.index(job) - 1]

                def high_part(w, v, start):
                    mm(to, w[0], v[0], start=start, stop=False)
                    mm(to, w[1], v[0], start=False, stop=False)

                if k == 0:
                    if gate == "i":
                        wait(pe, (prev, "low"), g, h)
                        if job == LSTM_JOBS[2]:
                            pe.wait_ge(sem_split, 1)
                    high_part(w_in, seen, True)
                    signal(mm(to, w_in[0], seen[1], start=False, stop=True), op, h)
                elif what == "input":
                    if gate == "o":
                        wait(pe, (job, "act", "i"), g, h)
                    else:
                        wait(pe, (prev, "act", bank_reader(prev, gate)), g, h)
                    high_part(w_in, seen, True)
                    mm(to, w_in[0], seen[1], start=False, stop=False)
                elif what == "high":
                    if gate == "i":
                        wait(pe, (prev, "high"), g, h)
                    high_part(w_rec, state, False)
                else:
                    if gate == "i":
                        wait(pe, (prev, "low"), g, h)
                    if gate in "fo":
                        high_part(w_rec, state, False)
                    signal(mm(to, w_rec[0], state[1], start=False, stop=True), op, h)

            run(pe, "PE", emit)

            with pe.Fori(0, CHUNKS // 2) as c:
                for h in range(2):
                    pe.wait_ge(z2_kept[h], c + 1)
                    pe.wait_ge(z2_bn[h], c + 1)
                    pe.wait_ge(r_ready[h], 2 * c + 2)
                    for j in range(2):
                        last = mm(gate_bank[h][0][:], gw2_sb[:, j, :],
                                  z[:, bass.ds(2 * c + h, 1), j, :].rearrange("p o n -> p (o n)"),
                                  start=(j == 0), stop=(j == 1))
                    last.then_inc(z2_full[h], 1)

            with pe.Fori(0, GROUPS) as g:
                for h in range(2):
                    pe.wait_ge(y_res[h], 2 * g + 1)
                    for n in range(2):
                        pe.wait_ge(y_scaled[h], 2 * g + n + 1)
                        for b in range(4):
                            last = nc.tensor.transpose(gate_bank[h][n][:, b * P:(b + 1) * P],
                                                       scaled[h][:, n, b * P:(b + 1) * P], ident[:])
                        last.then_inc(y_full[h], 1)

        @block.scalar
        def _(act):
            activation = nc.scalar.activation

            def emit(op, g, h):
                if isinstance(op[0], tuple):
                    job, what = op[0:2]
                    n = columns_of(job)
                    if what == "act":
                        gate = op[2]
                        p = job[1]
                        wait(act, (job, "gate", gate), g, h)
                        if gate == "i" and job == LSTM_JOBS[0]:
                            act.wait_ge(sem_setup, 1)
                        if gate == "o" and job == LSTM_JOBS[0]:
                            wait_earlier(act, (LSTM_JOBS[-1], "hidden"), g, h, 2)
                        if gate == "o" and job == LSTM_JOBS[1]:
                            wait(act, (LSTM_JOBS[0], "hidden"), g, h)
                        ins = activation(acts[gate][h][:, 0:n], gate_bank[h][bank_of(job, gate)][:, 0:n],
                                         ACT.Tanh if gate == "g" else ACT.Sigmoid,
                                         bias=lstm_bias[:, p - 1, GATE_AT[gate]:GATE_AT[gate] + 1],
                                         scale=1.0 if p == 1 else 1.0 / (W_SCALE * H_SCALE))
                    else:
                        wait(act, (job, "cell" if "f" in gates_of(job) else "new"), g, h)
                        ins = activation(acts["f"][h][:, 0:n], cell[h][:, 0:n], ACT.Tanh)
                elif op[0] == "back":
                    _, what, n = op
                    if what == "mixed":
                        wait(act, ("back", "mix", n, 3), g, h)
                        ins = activation(rows[:, n, :], back_bank[:], ACT.Copy)
                    else:
                        wait(act, ("back", "z", n), g, h)
                        at = z[:, bass.ds(4 * g + (2 * h + n // 2), 1), n % 2, :].rearrange("p o n -> p (o n)")
                        ins = activation(at, back_bank[:], ACT.Identity, bias=v1_sb[:, 0, n % 2:n % 2 + 1])
                else:
                    stage, _, n = op
                    if stage == "mix0":
                        wait(act, (stage, "product", n, 3), g, h)
                        ins = activation(mixed[:, n, :], front_bank[:], ACT.Copy)
                    elif stage == "lin0":
                        wait(act, (stage, "biased", n), g, h)
                        ins = activation(h0T[:, n, :], h0T[:, n, :], ACT.Relu)
                    else:
                        wait(act, (stage, "product", n, 3), g, h)
                        wait_earlier(act, (LSTM_JOBS[n], "gate", "o"), g, h, 1)
                        ins = activation(h1T[:, n, :], front_bank[:], ACT.Relu)
                signal(ins, op, h)

            run(act, "ACT", emit)

            wait(act, ("back", "z_stored", 3), GROUPS - 1, 1)
            act.wait_ge(sem_loaded, 16 * LOADS)
            act.wait_ge(sem_bn1, 5)
            with act.Fori(0, CHUNKS // 2) as c:
                for h in range(2):
                    for j in range(2):
                        at = z[:, bass.ds(2 * c + h, 1), j, :].rearrange("p o n -> p (o n)")
                        activation(at, at, ACT.Relu, bias=small[:, 10 + j:11 + j], scale=small[:, 8 + j:9 + j]
                                   ).then_inc(r_ready[h], 1)

            act.wait_ge(sem_bn2, 5)
            with act.Fori(0, GROUPS) as g:
                for h in range(2):
                    act.wait_ge(y_full[h], 2 * g + 1)
                    for n in range(2):
                        activation(scaled[h][:, n, :],
                                   z[:, bass.ds(4 * g + 2 * h + n, 1), 0, :].rearrange("p o n -> p (o n)"),
                                   ACT.Identity, bias=small[:, 2:3], scale=small[:, 1:2]
                                   ).then_inc(y_scaled[h], 1)

        @block.vector
        def _(dve):
            ve = nc.vector
            dve.wait_ge(sem_first, 16 * FIRST_LOADS)
            dve.wait_ge(sem_ident, 3)
            scratch = normed_sb
            ve.tensor_copy(ident16[:], ident[:])
            ve.tensor_tensor(scratch[:, 0, 0:P], adj_sb[:], ident[:], ALU.mult)
            ve.tensor_tensor(scratch[:, 0, P:2 * P], adj_sb[:], adjT_sb[:], ALU.add)
            ve.tensor_tensor(adj_sb[:], adj_sb[:], ident[:], ALU.add).then_inc(sem_degree, 1)
            dve.wait_ge(sem_degree, 1)
            ve.tensor_tensor(scratch[:, 1, 0:P], scratch[:, 0, P:2 * P], scratch[:, 0, 0:P], ALU.subtract
                             ).then_inc(sem_degree, 1)
            dve.wait_ge(sem_degree, 2)
            ve.reduce_sum(small[:, 1:2], scratch[:, 1, 0:P], mybir.AxisListType.X).then_inc(sem_degree, 1)
            dve.wait_ge(sem_degree, 3)
            ve.tensor_scalar_add(small[:, 2:3], small[:, 1:2], 1.0).then_inc(sem_degree, 1)
            dve.wait_ge(sem_setup_pe, 1)
            ve.tensor_copy(bias0[:], back_bank[:, 0:P]).then_inc(sem_degree, 1)
            dve.wait_ge(sem_loaded, 16 * LOADS)
            ve.tensor_tensor(lstm_bias[:], lstm_bias[:], bhh_sb[:], ALU.add).then_inc(sem_setup, 1)
            dve.wait_ge(sem_setup_pool, 1)
            ve.tensor_scalar(normed_sb[:, 1, P:2 * P], ident[:], small[:, 3:4], None, ALU.mult).then_inc(sem_setup, 1)
            dve.wait_ge(sem_degree, 5)

            def over4(t):
                return t[:].unsqueeze(1).broadcast_to([P, 4, P])

            def prepare_back():
                dve.wait_ge(sem_wr, 16)
                ve.tensor_scalar(w_hi[:], w_stage, W_SCALE, None, ALU.mult).then_inc(sem_degree, 1)
                dve.wait_ge(sem_degree, 6)
                for s in range(3):
                    for m in range(2):
                        last = ve.scalar_tensor_tensor(out=w_lo[:, s, m, :], in0=w_stage[:, s, m, :], scalar=W_SCALE,
                                                       in1=w_hi[:, s, m, :], op0=ALU.mult, op1=ALU.subtract)
                last.then_inc(sem_split, 1)
                dve.wait_ge(sem_setup_pe, 2)
                ve.tensor_scalar(ahatT[:], back_bank[:, 0:P], small[:, 3:4], None, ALU.mult).then_inc(sem_ahat, 1)

            def emit(op, g, h):
                if isinstance(op[0], tuple):
                    lstm_state(op, g, h)
                elif op[0] == "back":
                    back_rows(op, g, h)
                else:
                    stage, _, n = op
                    wait(dve, (stage, "product", n, 0 if stage == "lin0" else 3), g, h)
                    dst, bias = (h0T, bias0) if stage == "lin0" else (mixed, bias1)
                    signal(ve.tensor_tensor(dst[:, n, :].rearrange("p (b n) -> p b n", n=P),
                                            front_bank[:].rearrange("p (b n) -> p b n", n=P), over4(bias), ALU.add),
                           op, h)
                    if op == ("lin1", "out", 1) and isinstance(g, int) and (g, h) == (0, 0):
                        prepare_back()

            def row_stats(t, bn_t, n):
                for b in range(4 * n, 4 * n + 4):
                    last = ve.bn_stats(bn_t[:, b, :], flat(t[:])[:, b * P:(b + 1) * P])
                return last

            def row_moments(bn_t, comb_t, veps_t, step):
                mean_e, m2_e, mean_o, m2_o = (bn_t[:, :, n] for n in (1, 2, 4, 5))
                apart, m2, mean = (comb_t[:, n, :] for n in range(3))
                if step == 0:
                    ve.tensor_tensor(apart, mean_e, mean_o, ALU.subtract)
                    ve.scalar_tensor_tensor(out=m2, in0=m2_e, scalar=P * EPS, in1=m2_o, op0=ALU.add, op1=ALU.add)
                    return ve.tensor_tensor(mean, mean_e, mean_o, ALU.add)
                if step == 1:
                    ve.tensor_scalar(mean, mean, 0.5, None, ALU.mult)
                    return ve.scalar_tensor_tensor(out=apart, in0=apart, scalar=0.25, in1=apart, op0=ALU.mult,
                                                   op1=ALU.mult)
                return ve.scalar_tensor_tensor(out=veps_t[:], in0=m2, scalar=1.0 / P, in1=apart, op0=ALU.mult,
                                               op1=ALU.add)

            def normalize(src, dst, comb_t, rstd_t, n):
                for b in range(4 * n, 4 * n + 4):
                    at = slice(b * P, (b + 1) * P)
                    last = ve.tensor_scalar(flat(dst[:])[:, at], flat(src[:])[:, at], comb_t[:, 2, b:b + 1],
                                            rstd_t[:, b:b + 1], ALU.subtract, ALU.mult)
                return last

            def back_rows(op, g, h):
                _, what, n = op
                if what == "residual":
                    wait(dve, ("back", "tokens", n, 1), g, h)
                    if n == 0:
                        dve.wait_ge(sem_xb, loads(g, h))
                    ins = ve.scalar_tensor_tensor(out=rows[:, n, :], in0=back_bank[:], scalar=1.0 / H_SCALE,
                                                  in1=rows[:, n, :], op0=ALU.mult, op1=ALU.add)
                elif what == "stats":
                    wait(dve, ("back", "residual", n), g, h)
                    ins = row_stats(rows, bn[0], n)
                elif what == "moments":
                    wait(dve, ("back", "moments", n - 1) if n else ("back", "stats", 1), g, h)
                    ins = row_moments(bn[0], comb[0], veps[0], n)
                elif what == "normed":
                    if n == 0:
                        wait(dve, ("back", "rstd"), g, h)
                        if isinstance(g, int):
                            if 2 * g + h > 0:
                                dve.wait_ge(sem_kept, 16 * (2 * g + h))
                        else:
                            dve.wait_ge(sem_kept, loads(g, h, -16))
                    ins = normalize(rows, normed[0], comb[0], rstd[0], n)
                else:
                    wait(dve, ("back", "z_stored", n), g, h)
                    at = z_moments[:, n % 2, bass.ds(4 * g + (2 * h + n // 2), 1), :].rearrange("p o s -> p (o s)")
                    ins = ve.bn_stats(at, back_bank[:])
                signal(ins, op, h)

            def lstm_state(op, g, h):
                job, what = op
                _, p, k = job
                n = columns_of(job)
                i, gg, f, o = (acts[name][h][:, 0:n] for name in "igfo")
                c = cell[h][:, 0:n]
                if what == "new":
                    wait(dve, (job, "act", "g"), g, h)
                    ins = ve.tensor_tensor(i if "f" in gates_of(job) else c, i, gg, ALU.mult)
                elif what == "kept":
                    wait(dve, (job, "act", "f"), g, h)
                    ins = ve.tensor_tensor(c, c, f, ALU.mult)
                elif what == "cell":
                    wait(dve, (job, "kept"), g, h)
                    ins = ve.tensor_tensor(c, c, i, ALU.add)
                elif what == "hidden":
                    wait(dve, (job, "tanh"), g, h)
                    ins = ve.scalar_tensor_tensor(out=f, in0=o, scalar=H_SCALE, in1=f, op0=ALU.mult, op1=ALU.mult)
                else:
                    if p == 1:
                        hi, lo = (t[h][:, 4 * k:4 * k + 4, :].rearrange("p b t -> p (b t)") for t in (h_hi, h_lo))
                    elif k < p - 1:
                        hi, lo = s_hi[h][:, 0:n], s_lo[h][:, 0:n]
                    else:
                        hi, lo = window(h_hi[h], p, k), window(h_lo[h], p, k)
                        f = f.rearrange("p (b w) -> p b w", b=GB)
                    if what == "high":
                        wait(dve, (job, "hidden"), g, h)
                        if job == LSTM_JOBS[0]:
                            wait_earlier(dve, ("back", "tokens", 1, 1), g, h, 2)
                        ins = ve.tensor_copy(hi, f)
                    else:
                        wait(dve, (job, "high"), g, h)
                        ins = ve.tensor_tensor(lo, f, hi, ALU.subtract)
                signal(ins, op, h)

            run(dve, "DVE", emit)

            wait(dve, ("back", "z_stats", 3), GROUPS - 1, 1)
            for j in range(2):
                last = ve.bn_aggr(mv[:, j, :], z_moments[:, j, :, :].rearrange("p c s -> p (c s)"))
            last.then_inc(sem_bn1, 1)
            dve.wait_ge(sem_bn1, 1)
            ve.tensor_tensor(small[:, 14:16], mv[:, 0:2, 0], v1_sb[:, 0, :], ALU.add)
            ve.tensor_scalar_add(small[:, 4:6], mv[:, 0:2, 1], EPS).then_inc(sem_bn1, 1)
            dve.wait_ge(sem_bn1_pow, 1)
            ve.tensor_tensor(small[:, 8:10], small[:, 6:8], v1_sb[:, 1, :], ALU.mult).then_inc(sem_bn1, 1)
            dve.wait_ge(sem_bn1, 3)
            ve.tensor_tensor(small[:, 14:16], small[:, 14:16], small[:, 8:10], ALU.mult).then_inc(sem_bn1, 1)
            dve.wait_ge(sem_bn1, 4)
            ve.tensor_tensor(small[:, 10:12], v1_sb[:, 2, :], small[:, 14:16], ALU.subtract).then_inc(sem_bn1, 1)

            with dve.Fori(0, CHUNKS // 2) as c:
                for h in range(2):
                    dve.wait_ge(z2_full[h], c + 1)
                    ve.bn_stats(bn[h][:, 0, :], gate_bank[h][0][:]).then_inc(z2_bn[h], 1)
                    ve.tensor_scalar(z[:, bass.ds(2 * c + h, 1), 0, :].rearrange("p o n -> p (o n)"),
                                     gate_bank[h][0][:], v2_sb[:, 0:1], None, ALU.add).then_inc(z2_kept[h], 1)
                    dve.wait_ge(z2_bn[h], c + 2)
                    ve.tensor_copy(z_moments[:, 0, bass.ds(2 * c + h, 1), :].rearrange("p o s -> p (o s)"),
                                   bn[h][:, 0, :]).then_inc(z2_moments[h], 1)

            for h in range(2):
                dve.wait_ge(z2_moments[h], CHUNKS // 2)
                dve.wait_ge(z2_kept[h], CHUNKS // 2 + 1)
            ve.bn_aggr(mv[:, 0, :], z_moments[:, 0, :, :].rearrange("p c s -> p (c s)")).then_inc(sem_bn2, 1)
            dve.wait_ge(sem_bn2, 1)
            ve.tensor_tensor(small[:, 14:15], mv[:, 0, 0:1], v2_sb[:, 0:1], ALU.add)
            ve.tensor_scalar_add(small[:, 12:13], mv[:, 0, 1:2], EPS).then_inc(sem_bn2, 1)
            dve.wait_ge(sem_bn2_pow, 1)
            ve.tensor_tensor(small[:, 1:2], small[:, 13:14], v2_sb[:, 1:2], ALU.mult).then_inc(sem_bn2, 1)
            dve.wait_ge(sem_bn2, 3)
            ve.tensor_tensor(small[:, 15:16], small[:, 14:15], small[:, 1:2], ALU.mult).then_inc(sem_bn2, 1)
            dve.wait_ge(sem_bn2, 4)
            ve.tensor_tensor(small[:, 2:3], v2_sb[:, 2:3], small[:, 15:16], ALU.subtract).then_inc(sem_bn2, 1)

            with dve.Fori(0, GROUPS) as g:
                for h in range(2):
                    dve.wait_ge(x1_back[h], 16 * g + 16)
                    dve.wait_ge(y_out[h], 16 * g + 1)
                    for n in range(2):
                        dve.wait_ge(y_full[h], 2 * g + n + 2)
                        ve.tensor_tensor(normed[h][:, n, :], gate_bank[h][n][:], x1_again[h][:, n, :], ALU.add
                                         ).then_inc(y_res[h], 1)
                    for n in range(2):
                        dve.wait_ge(y_res[h], 2 * g + n + 2)
                        last = row_stats(normed[h], bn[h], n)
                    last.then_inc(y_mom[h], 1)
                    for step in range(3):
                        dve.wait_ge(y_mom[h], 4 * g + step + 1)
                        row_moments(bn[h], comb[h], veps[h], step).then_inc(y_mom[h], 1)
                    dve.wait_ge(y_rstd[h], g + 1)
                    for n in range(2):
                        last = normalize(normed[h], normed[h], comb[h], rstd[h], n)
                    last.then_inc(y_norm[h], 1)
        return nc


INPUTS = ("x", "adj", "adjT", "w0", "b0_rep", "w1", "b1_rep", "wih1", "b_ih", "b_hh", "wr", "gw1", "gw2",
          "vec1", "vec2")


def kernel(**inputs):
    import concourse.bacc as bacc
    from concourse.bass_utils import run_bass_kernel_spmd

    a = {k: np.asarray(v) for k, v in inputs.items()}
    x = a["x"]
    nb = x.shape[0]
    wih, whh = a["L0_gnn_Wih"], a["L0_gnn_Whh"]
    laid = {
        "x": x.reshape(nb // GB, GB, P, P).transpose(0, 2, 1, 3).reshape(nb // GB, P, GB * P),
        "adj": a["adj"],
        "adjT": a["adj"].T,
        "w0": a["L0_gnn_Wg0"],
        "b0_rep": np.broadcast_to(a["L0_gnn_bg0"][None, :], (P, P)),
        "w1": a["L0_gnn_Wg1"],
        "b1_rep": np.broadcast_to(a["L0_gnn_bg1"][None, :], (P, P)),
        "wih1": np.stack([wih[0, GATE_AT[n] * P:(GATE_AT[n] + 1) * P].T for n in GATES_FIRST], axis=1),
        "b_ih": a["L0_gnn_bih"].reshape(4, 4, P).transpose(2, 0, 1),
        "b_hh": a["L0_gnn_bhh"].reshape(4, 4, P).transpose(2, 0, 1),
        "wr": np.stack([wih[1:], whh[1:]], axis=1).transpose(3, 0, 1, 2),
        "gw1": a["L1_gnn_W1"].reshape(2, P, P).transpose(2, 0, 1),
        "gw2": a["L1_gnn_W2"].reshape(P, 2, P).transpose(2, 1, 0),
        "vec1": np.stack([a[f"L1_gnn_{n}"].reshape(2, P).T for n in ("b1", "g1", "be1")], axis=1),
        "vec2": np.stack([a[f"L1_gnn_{n}"] for n in ("b2", "g2", "be2")], axis=1),
    }
    nc = bacc.Bacc("TRN2", target_bir_lowering=False, num_devices=1)
    arrays, args = {}, []
    for name in INPUTS:
        arrays[f"in_{name}"] = np.ascontiguousarray(laid[name])
        args.append(nc.dram_tensor(f"in_{name}", arrays[f"in_{name}"].shape, F32, kind="ExternalInput").ap())
    out = nc.dram_tensor("out", (nb // GB, P, GB * P), F32, kind="ExternalOutput").ap()
    gnn_lstm_kernel(nc, *args, out)
    result = run_bass_kernel_spmd(nc, [arrays], core_ids=[0]).results[0]["out"]
    return result.reshape(nb // GB, P, GB, P).transpose(0, 2, 1, 3).reshape(nb, P, P)
```

```python
from contextlib import ExitStack

import numpy as np

import concourse.bass as bass
from concourse import mybir

F32 = mybir.dt.float32
F16 = mybir.dt.float16
ALU = mybir.AluOpType
ACT = mybir.ActivationFunctionType

P = 128
BANK = 512
EPS = 1e-5
GB = 8
SKIPS = (2, 3, 4)
W_SCALE = 2.0 ** 6
A_SCALE = 2.0 ** 4
H_SCALE = 2.0 ** 14
GATES_FIRST = ("i", "g", "o")
GATES_NEXT = ("i", "g", "f", "o")
GATE_AT = {"i": 0, "f": 1, "g": 2, "o": 3}

LSTM_JOBS = [("lstm", 1, c) for c in range(2)] + [("lstm", p, k) for p in SKIPS for k in range(p)]


def gates_of(job):
    return GATES_FIRST if job[1] == 1 or job[2] == 0 else GATES_NEXT


def columns_of(job):
    return BANK if job[1] == 1 else GB * (P // job[1])


def matmul_us(columns, passes):
    return passes * (columns / 2.4 + 2.5) / 1e3


MIX_US = 2 * matmul_us(2 * P, 1)
WIDE_US = 2 * matmul_us(2 * BANK, 1)


def vector_us(columns, rate=1):
    return (77 + columns / rate) / 960 - 0.01


def scalar_us(columns, pointers):
    return (51 + 93 * pointers + columns / 1.2) / 1e3


FRONT_PAIRED = 3
BACK_WIDE = 2


def front_stage(paired=False):
    ops, bank_free = [], None
    for stage, parts, before in (("mix0", 4, None), ("lin0", 1, "mix0"), ("lin1", 4, "lin0"), ("mix1", 4, "lin1")):
        for n in range(2):
            after = [(before, "out", n)] if before else []
            after += [bank_free] if bank_free and not paired else []
            for i in range(parts):
                ops.append(("PE", (stage, "product", n, i), MIX_US if parts == 4 else WIDE_US,
                            after if i == 0 else []))
            after = [(stage, "product", n, parts - 1)]
            if stage == "lin0":
                ops.append(("DVE", (stage, "biased", n), vector_us(BANK), after))
                after = [(stage, "biased", n)]
            ops.append(("DVE", (stage, "out", n), vector_us(BANK), after) if stage == "lin1" else
                       ("ACT", (stage, "out", n), scalar_us(BANK, 0) + (0.04 if stage == "lin0" else 0), after))
            bank_free = (stage, "biased" if stage == "lin0" else "out", n)
    return ops


BANK_OF = {"i": 0, "g": 1, "f": 2, "o": 0}


def bank_of(job, gate):
    return 2 if gate == "o" and gates_of(job) == GATES_FIRST else BANK_OF[gate]


def bank_reader(job, gate):
    return [n for n in gates_of(job) if bank_of(job, n) == BANK_OF[gate]][-1]


def lstm_stage():
    ops, prev = [], None
    for job in LSTM_JOBS:
        n = columns_of(job)
        gates = gates_of(job)
        if job[1] == 1:
            for gate in gates:
                after = [("mix1", "out", job[2])] if gate == "i" else []
                after += [(prev, "act", gate)] if job[2] == 1 else []
                ops.append(("PE", (job, "gate", gate), WIDE_US, after))
        elif job[2] == 0:
            for gate in gates:
                ops.append(("PE", (job, "gate", gate), matmul_us(n, 3), [(prev, "low")]))
        else:
            for gate in "igf":
                ops.append(("PE", (job, "input", gate), matmul_us(n, 3), [(prev, "act", bank_reader(prev, gate))]))
            for gate in "ig":
                ops.append(("PE", (job, "high", gate), matmul_us(n, 2), [(prev, "high")]))
            for gate in "ig":
                ops.append(("PE", (job, "gate", gate), matmul_us(n, 1), [(prev, "low")]))
            ops.append(("PE", (job, "gate", "f"), matmul_us(n, 3), []))
            ops.append(("PE", (job, "input", "o"), matmul_us(n, 3), [(job, "act", "i")]))
            ops.append(("PE", (job, "gate", "o"), matmul_us(n, 3), []))
        for gate in gates:
            ops.append(("ACT", (job, "act", gate), scalar_us(n, 1), [(job, "gate", gate)]))
            if gate == "g":
                ops.append(("DVE", (job, "new"), vector_us(n), [(job, "act", "g")]))
            if gate == "f":
                ops.append(("DVE", (job, "kept"), vector_us(n), [(job, "act", "f")]))
                ops.append(("DVE", (job, "cell"), vector_us(n), [(job, "kept")]))
        ops.append(("ACT", (job, "tanh"), scalar_us(n, 0) + 0.04, [(job, "cell" if "f" in gates else "new")]))
        ops.append(("DVE", (job, "hidden"), vector_us(n), [(job, "tanh")]))
        ops.append(("DVE", (job, "high"), vector_us(n, 2), [(job, "hidden")]))
        ops.append(("DVE", (job, "low"), vector_us(n), [(job, "high")]))
        prev = job
    return ops


def back_stage(wide=False):
    ops = []
    for n in range(2):
        for i in range(2):
            after = [("back", "residual", 0)] if n and not wide else [(LSTM_JOBS[-1], "low")]
            ops.append(("PE", ("back", "tokens", n, i), matmul_us(P, 4), after if i == 0 else []))
        ops.append(("DVE", ("back", "residual", n), vector_us(BANK), [("back", "tokens", n, 1)]))
    for n in range(2):
        ops.append(("DVE", ("back", "stats", n), 0.81, [("back", "residual", n)]))
    for n in range(3):
        ops.append(("DVE", ("back", "moments", n), (0.25, 0.15, 0.08)[n],
                    [("back", "moments", n - 1) if n else ("back", "stats", 1)]))
    ops.append(("POOL", ("back", "rstd"), 1.62, [("back", "moments", 2)]))
    for n in range(2):
        ops.append(("DVE", ("back", "normed", n), 1.02, [("back", "rstd")]))
    for n in range(2):
        for i in range(4):
            after = [("back", "normed", n)] + ([("back", "mixed_low", 0)] if n and not wide else [])
            ops.append(("PE", ("back", "mix", n, i), MIX_US, after if i == 0 else []))
        ops.append(("ACT", ("back", "mixed", n), scalar_us(BANK, 0), [("back", "mix", n, 3)]))
        ops.append(("DVE", ("back", "mixed_low", n), vector_us(BANK), [("back", "mixed", n)]))
    for n in range(4):
        after = ("back", "mixed_low", min(n, 1)) if wide else ("back", "z_stats", n - 1) if n else ("back", "mixed_low", 1)
        ops.append(("PE", ("back", "z", n), matmul_us(BANK, 3), [after]))
        ops.append(("ACT", ("back", "z_stored", n), scalar_us(BANK, 1), [("back", "z", n)]))
        ops.append(("DVE", ("back", "z_stats", n), vector_us(BANK), [("back", "z_stored", n)]))
    return ops


def signal_of(op):
    what = op[1]
    if isinstance(op[0], tuple):
        return {"gate": "gates_full", "act": "gate_ready", "tanh": "tanh_cell", "new": "cell_part",
                "kept": "cell_part", "cell": "cell_part", "hidden": "hidden_part", "high": "hidden_part",
                "low": "hidden_part", "input": None}[what] if not (what == "high" and len(op) == 3) else None
    if op[0] == "back":
        return {"tokens": "back_product", "mix": "back_product", "z": "back_product", "rstd": "rstd",
                "residual": "residual", "stats": "moments", "moments": "moments", "normed": "normed",
                "mixed": "mixed", "mixed_low": "mixed_low", "z_stored": "z_stored", "z_stats": "z_stats"}[what]
    if what == "product":
        return "front_product"
    return "front_biased" if what == "biased" or op[0] == "lin1" else "front_out"


def count_signals():
    total, at = {}, {}
    for _, op, _, _ in front_stage() + lstm_stage() + back_stage():
        name = signal_of(op)
        if name:
            total[name] = total.get(name, 0) + 1
            at[op] = total[name]
    return total, at


EARLIER = {
    ("mix0", "product", 0, 0): (1, ("mix1", "out", 1)),
    ("mix1", "out", 0): (1, (LSTM_JOBS[0], "gate", "o")),
    ("mix1", "out", 1): (1, (LSTM_JOBS[1], "gate", "o")),
    (LSTM_JOBS[0], "gate", "i"): (2, (LSTM_JOBS[-1], "act", "o")),
    (LSTM_JOBS[0], "act", "o"): (2, (LSTM_JOBS[-1], "hidden")),
    (LSTM_JOBS[0], "high"): (2, ("back", "tokens", 1, 1)),
    ("back", "tokens", 0, 0): (1, ("back", "z_stats", 3)),
}


SIGNAL_US = {"PE": {"ACT": 0.21, "DVE": 0.2}, "ACT": {"PE": 0.29, "DVE": 0.16},
             "DVE": {"PE": 0.18, "DVE": 0.13, "ACT": 0.13, "POOL": 0.16}, "POOL": {"DVE": 0.2}}


AHEAD = {("DVE", "odd"): 0.1, ("DVE", "even"): 0.1, ("DVE", "front"): 0.3, ("DVE", "back"): -0.15,
         ("ACT", "back"): 0.4}
AHEAD_KIND = {("ACT", "mix0", "out"): 0.75, ("ACT", "lin0", "out"): -0.05, ("ACT", "lstm", 3): 0.05,
              ("ACT", "back", "z_stored"): -0.15, ("DVE", "back", "residual"): 0.1, ("DVE", "back", "stats"): 0.05}
AHEAD_LAST = {("back", 3): 0.15, ("front", 1): 0.1, ("back", 1): -0.2, ("front", 0): -0.05, ("odd", 0): -0.05}


def ahead(engine, stream, op, from_last):
    kind = op[0][0:2] if isinstance(op[0], tuple) else op[0:2]
    return (AHEAD.get((engine, stream), 0) + AHEAD_KIND.get((engine, *kind), 0)
            + AHEAD_LAST.get((stream, from_last), 0))


def plan_order(halves):
    streams = {"front": (lambda q: front_stage(q < FRONT_PAIRED), range(halves)),
               "even": (lambda q: lstm_stage(), range(0, halves, 2)),
               "odd": (lambda q: lstm_stage(), range(1, halves, 2)),
               "back": (lambda q: back_stage(q >= halves - BACK_WIDE), range(halves))}
    rank = {"front": 0, "back": 1, "even": 2, "odd": 2}
    engines = ("PE", "ACT", "DVE", "POOL")
    queue = {(s, e): [(q, *o[1:]) for q in qs for o in stage(q) if o[0] == e]
             for s, (stage, qs) in streams.items() for e in engines}
    at = dict.fromkeys(queue, 0)
    done, free, order = {}, dict.fromkeys(engines, 0.0), {e: [] for e in engines}
    while True:
        best = None
        for e in engines:
            for s in streams:
                if at[s, e] >= len(queue[s, e]):
                    continue
                q, op, us, after = queue[s, e][at[s, e]]
                needs = [(q, x) for x in after]
                if op in EARLIER and q >= EARLIER[op][0]:
                    needs.append((q - EARLIER[op][0], EARLIER[op][1]))
                if (q, op) == (0, ("back", "tokens", 0, 0)):
                    needs.append((FRONT_PAIRED - 1, ("mix1", "out", 1)))
                if any(x not in done for x in needs):
                    continue
                start = max([free[e]] + [done[x][0] + SIGNAL_US[done[x][1]][e] for x in needs])
                key = (round(start - ahead(e, s, op, halves - 1 - q), 4), rank[s], q)
                if best is None or key < best[0]:
                    best = (key, e, s, q, op, start, us)
        if best is None:
            return order
        _, e, s, q, op, start, us = best
        free[e] = start + us
        done[q, op] = free[e], e
        at[s, e] += 1
        order[e].append((start, q, op))


def cut_order(halves):
    order = plan_order(halves)
    cuts = [t for t, q, op in order["PE"] if op == ("mix0", "product", 0, 0) and q % 2 == 0]
    chunks = {e: [[(q - 2 * k, op) for t, q, op in ops
                   if (k == 0 or t >= cuts[k]) and (k + 1 == len(cuts) or t < cuts[k + 1])]
                  for k in range(len(cuts))] for e, ops in order.items()}
    runs = [(k0, k1) for k0 in range(1, len(cuts)) for k1 in range(k0 + 1, len(cuts))
            if all(c[k] == c[k0] for c in chunks.values() for k in range(k0, k1))
            and all(q + 2 * k0 >= EARLIER.get(op, (0,))[0] for c in chunks.values() for q, op in c[k0])]
    return chunks, max(runs, key=lambda r: r[1] - r[0])


def gnn_lstm_kernel(nc, x, adj, adjT, w0, b0_rep, w1, b1_rep, wih1, b_ih, b_hh, wr, gw1, gw2, vec1, vec2, out):
    HALVES = x.shape[0]
    GROUPS = HALVES // 2
    HW = GB * P
    CHUNKS = HALVES * 2
    PER, AT = count_signals()
    CHUNK_OF, (LOOP_FROM, LOOP_TO) = cut_order(HALVES)

    x1_dram = nc.dram_tensor("x1_kept", [HALVES, P, HW], F32, kind="Internal").ap()

    with ExitStack() as ctx:
        def sb(name, shape, dt=F32):
            return ctx.enter_context(nc.sbuf_tensor(name, shape, dt))

        def sem(name):
            return ctx.enter_context(nc.semaphore(name))

        adj_sb = sb("adj_sb", [P, P])
        adjT_sb = sb("adjT_sb", [P, P])
        ahatT = sb("ahatT", [P, P])
        ident = sb("ident", [P, P])
        ident16 = sb("ident16", [P, P], F16)
        w0_sb = sb("w0_sb", [P, P])
        w1_sb = sb("w1_sb", [P, P])
        bias0 = sb("bias0", [P, P])
        bias1 = sb("bias1", [P, P])
        wih1_sb = sb("wih1_sb", [P, 3, P])
        w_hi = sb("w_hi", [P, len(SKIPS), 2, 4 * P], F16)
        w_lo = sb("w_lo", [P, len(SKIPS), 2, 4 * P], F16)
        lstm_bias = sb("lstm_bias", [P, 4, 4])
        bhh_sb = sb("bhh_sb", [P, 4, 4])
        gw1_hi = sb("gw1_hi", [P, 2, P], F16)
        gw1_lo = sb("gw1_lo", [P, 2, P], F16)
        gw2_sb = sb("gw2_sb", [P, 2, P])
        v1_sb = sb("v1_sb", [P, 3, 2])
        v2_sb = sb("v2_sb", [P, 3])
        small = sb("small", [P, 16])
        neg_half = sb("neg_half", [P, GB])

        z = sb("z", [P, CHUNKS, 2, BANK])
        z_moments = sb("z_moments", [P, 2, CHUNKS, 6])

        x_front = sb("x_front", [P, 2, BANK])
        mixed = sb("mixed", [P, 2, BANK])
        h0T = sb("h0T", [P, 2, BANK])
        h1T = sb("h1T", [P, 2, BANK])

        def two(name, shape, dt=F32):
            return [sb(f"{name}{h}", shape, dt) for h in range(2)]

        h_hi = two("h_hi", [P, GB, P], F16)
        h_lo = two("h_lo", [P, GB, P], F16)
        s_hi = two("s_hi", [P, BANK], F16)
        s_lo = two("s_lo", [P, BANK], F16)
        acts = {n: two(f"gate_{n}", [P, BANK]) for n in "igfo"}
        cell = two("cell", [P, BANK])

        rows_sb = sb("rows_sb", [P, 2, BANK])
        normed_sb = sb("normed_sb", [P, 2, BANK])
        rows = rows_sb
        normed = normed_sb
        scaled = [mixed, h0T, x_front, rows_sb]
        bn, comb, veps, rstd, mean_rstd = (
            [sb(f"{name}{u}", [P, *shape], F32) for u in range(4)]
            for name, shape in (("bn", (GB, 6)), ("comb", (3, GB)), ("veps", (GB,)), ("rstd", (GB,)),
                                ("mean_rstd", (GB,))))
        mv = sb("mv", [P, 2, 2])
        w_stage = z[:, 0:len(SKIPS), :, :]
        gw1_stage = z[:, len(SKIPS), 0, 0:2 * P].rearrange("p (j n) -> p j n", j=2)

        gate_bank = [[ctx.enter_context(nc.psum_tensor(f"gate_bank{h}{n}", [P, BANK], F32)) for n in range(3)]
                     for h in range(2)]
        front_bank = ctx.enter_context(nc.psum_tensor("front_bank", [P, BANK], F32))
        back_bank = ctx.enter_context(nc.psum_tensor("back_bank", [P, BANK], F32))
        setup_bank = gate_bank[1][2]
        row_bank = [gate_bank[0][0:2], gate_bank[1][0:2], [gate_bank[0][2], gate_bank[1][2]],
                    [front_bank, back_bank]]

        sem_adjT = sem("adjT_loaded")
        sem_first = sem("first_weights_loaded")
        sem_loaded = sem("weights_loaded")
        sem_wr = sem("recurrent_weights_loaded")
        sem_ident = sem("ident_ready")
        sem_zeros = sem("zeros_ready")
        sem_setup = sem("setup_step")
        sem_degree = sem("degree_step")
        sem_setup_pe = sem("setup_product")
        sem_setup_pool = sem("setup_pow")
        sem_ahat = sem("ahat_ready")
        sem_split = sem("weights_split")
        sem_x = sem("x_front_loaded")
        sem_xb = sem("x_back_loaded")
        sem_kept = sem("x1_kept")
        lstm_signals = ("gates_full", "gate_ready", "tanh_cell", "cell_part", "hidden_part")
        S = {name: [sem(f"{name}{h}") for h in range(2)] if name in lstm_signals else sem(name) for name in PER}
        sem_bn1 = sem("bn1_step")
        sem_bn1_pow = sem("bn1_pow")
        r_ready = [sem(f"r_ready{h}") for h in range(2)]
        z2_full = [sem(f"z2_full{h}") for h in range(2)]
        z2_kept = [sem(f"z2_kept{h}") for h in range(2)]
        sem_bn2 = sem("bn2_step")
        sem_bn2_pow = sem("bn2_pow")
        y_scaled = [[sem(f"y_scaled{n}{u}") for u in range(4)] for n in range(2)]
        x1_back = sem("x1_back")
        y_full = [sem(f"y_full{u}") for u in range(4)]
        y_mom = [sem(f"y_moments{u}") for u in range(4)]
        y_rstd = [sem(f"y_rstd{u}") for u in range(4)]
        y_norm = [sem(f"y_normed{u}") for u in range(4)]
        y_last = sem("y_last_normed")
        y_out = sem("y_stored")
        y_shift = [sem(f"y_shift{u}") for u in range(4)]

        def signal(ins, op, h):
            name = signal_of(op)
            ins.then_inc(S[name][h] if name in lstm_signals else S[name], 1)

        def wait(eng, op, g, h):
            name = signal_of(op)
            if name in lstm_signals:
                eng.wait_ge(S[name][h], g * PER[name] + AT[op])
            else:
                eng.wait_ge(S[name], g * (2 * PER[name]) + (h * PER[name] + AT[op]))

        def wait_earlier(eng, op, g, h, by):
            h_then = (h - by) % 2
            g_then = g + (h - by) // 2 if (h - by) // 2 else g
            if not (isinstance(g_then, int) and g_then < 0):
                wait(eng, op, g_then, h_then)

        def loads(g, h, extra=0):
            return g * 32 + (16 * h + 16 + extra)

        def run(eng, engine, emit):
            def chunk(k, at):
                for q, op in CHUNK_OF[engine][at]:
                    emit(op, k + q // 2 if q // 2 else k, q % 2)
            for k in range(LOOP_FROM):
                chunk(k, k)
            with eng.Fori(LOOP_FROM, LOOP_TO) as k:
                chunk(k, LOOP_FROM)
            for k in range(LOOP_TO, len(CHUNK_OF[engine])):
                chunk(k, k)

        def paired(g, h):
            return isinstance(g, int) and 2 * g + h < FRONT_PAIRED

        def wide(g, h):
            return isinstance(g, int) and 2 * g + h >= HALVES - BACK_WIDE

        def agg(n):
            both = rows[:, n, :].bitcast(F16)
            return both[:, 0:BANK], both[:, BANK:2 * BANK]

        def front_to(g, h, n):
            return back_bank if paired(g, h) and n == 1 else front_bank

        def back_to(g, h, n):
            return gate_bank[0][n - 1] if wide(g, h) and n else back_bank

        free_at_start = [z2_kept, y_full, y_norm]
        FIRST_LOADS, LOADS = 4, 8
        STAY_WARM = 20
        TURN = 8
        WARM_UP = 8
        block = ctx.enter_context(nc.Block())

        def scale_z2(eng, n, t, u):
            eng.wait_ge(y_full[u], 2 * t + 1)
            eng.tensor_scalar(scaled[u][:, n, :],
                              z[:, bass.ds(8 * t + (2 * u + n), 1), 0, :].rearrange("p o n -> p (o n)"),
                              small[:, 1:2], small[:, 2:3], ALU.mult, ALU.add).then_inc(y_scaled[n][u], 1)

        def flat(t):
            return t.rearrange("p a n -> p (a n)")

        def half_of(dram, g, h):
            if isinstance(g, int):
                return dram[2 * g + h]
            return dram[bass.ds(2 * g + h, 1)].rearrange("o p n -> p (o n)")

        def x1_at(g, h):
            return z[:, bass.ds(4 * g + 2 * h, 2), 1, :]

        @block.sync
        def _(sp):
            sp.dma_start(adjT_sb[:], adjT).then_inc(sem_adjT, 16)
            sp.dma_start(flat(x_front[:]), x[0]).then_inc(sem_x, 16)
            for dst, src in ((adj_sb[:], adj), (w0_sb[:], w0), (bias0[:], b0_rep),
                             (w1_sb[:], w1)):
                sp.dma_start(dst, src).then_inc(sem_first, 16)
            for dst, src in ((bias1[:], b1_rep), (lstm_bias[:], b_ih), (bhh_sb[:], b_hh), (wih1_sb[:], wih1),
                             (gw1_stage, gw1), (gw2_sb[:], gw2), (v1_sb[:], vec1), (v2_sb[:], vec2)):
                sp.dma_start(dst, src).then_inc(sem_loaded, 16)
            sp.dma_start(w_stage, wr).then_inc(sem_wr, 16)
            sp.dma_start(flat(rows[:]), x[0]).then_inc(sem_xb, 16)

            def next_front(g, h):
                wait(sp, ("mix0", "product", 1, 3), g, h)
                g_next, h_next = (g, 1) if h == 0 else (g + 1, 0)
                sp.dma_start(flat(x_front[:]), half_of(x, g_next, h_next)).then_inc(sem_x, 16)

            def back(g, h, more=True):
                wait(sp, ("back", "normed", 1), g, h)
                sp.dma_start(half_of(x1_dram, g, h), flat(normed[:])).then_inc(sem_kept, 16)
                if more:
                    wait(sp, ("back", "z", 3), g, h)
                    g_next, h_next = (g, 1) if h == 0 else (g + 1, 0)
                    sp.dma_start(flat(rows[:]), half_of(x, g_next, h_next)).then_inc(sem_xb, 16)

            for q in range(4):
                next_front(q // 2, q % 2)
            back(0, 0)
            with sp.Fori(2, GROUPS - 1) as g:
                next_front(g, 0)
                back(g - 2, 1)
                next_front(g, 1)
                back(g - 1, 0)
            next_front(GROUPS - 1, 0)
            back(GROUPS - 3, 1)
            for q in range(HALVES - 4, HALVES):
                back(q // 2, q % 2, q + 1 < HALVES)

            sp.wait_ge(sem_kept, 16 * HALVES)
            with sp.Fori(0, GROUPS) as g:
                for h in range(2):
                    for c in range(2):
                        sp.wait_ge(z2_full[c], 2 * g + (h + 1))
                    sp.dma_start(x1_at(g, h), half_of(x1_dram, g, h).rearrange("p (a n) -> p a n", a=2)
                                 ).then_inc(x1_back, 16)
            def store(t, u):
                g, h = 2 * t + u // 2, u % 2
                sp.wait_ge(y_norm[u], t + 2)
                sp.dma_start(half_of(out, g, h).rearrange("p (a n) -> p a n", a=2), x1_at(g, h)).then_inc(y_out, 16)

            with sp.Fori(0, HALVES // 4 - 1) as t:
                for u in range(4):
                    store(t, u)
            for u in range(3):
                store(HALVES // 4 - 1, u)
            for n in range(2):
                sp.wait_ge(y_last, n + 1)
                sp.dma_start(out[HALVES - 1][:, n * BANK:(n + 1) * BANK], z[:, CHUNKS - 2 + n, 1, :]
                             ).then_inc(y_out, 16)
            sp.wait_ge(y_out, 16 * (HALVES + 1))

        @block.gpsimd
        def _(pool):
            for pair in free_at_start:
                for s in pair:
                    pool.sem_inc(s, 1)
            nc.gpsimd.memset(ident[:], 0.0).then_inc(sem_ident, 1)
            nc.gpsimd.memset(neg_half[:], -0.5).then_inc(sem_ident, 1)
            pool.wait_ge(sem_ident, 2)
            nc.gpsimd.affine_select(out=ident[:], in_=ident[:], compare_op=ALU.not_equal, fill=1.0, base=0,
                                    pattern=[[-1, P]], channel_multiplier=1).then_inc(sem_ident, 1)
            pool.wait_ge(sem_degree, 4)
            nc.gpsimd.tensor_tensor(small[:, 3:4], small[:, 2:3], neg_half[:, 0:1], ALU.pow).then_inc(sem_setup_pool, 1)

            def emit(op, g, h):
                wait(pool, ("back", "moments", 2), g, h)
                signal(nc.gpsimd.tensor_tensor(rstd[0][:], veps[0][:], neg_half[:], ALU.pow), op, h)

            run(pool, "POOL", emit)
            pool.wait_ge(sem_bn1, 2)
            nc.gpsimd.tensor_tensor(small[:, 6:8], small[:, 4:6], neg_half[:, 0:2], ALU.pow).then_inc(sem_bn1_pow, 1)
            pool.wait_ge(sem_bn2, 2)
            nc.gpsimd.tensor_tensor(small[:, 13:14], small[:, 12:13], neg_half[:, 0:1], ALU.pow).then_inc(sem_bn2_pow, 1)
            pool.wait_ge(sem_bn2, 5)
            for u in range(4):
                scale_z2(pool, 1, 0, u)

            def row_powers(t, u):
                pool.wait_ge(y_mom[u], 4 * t + 4)
                nc.gpsimd.tensor_tensor(rstd[u][:], veps[u][:], neg_half[:], ALU.pow).then_inc(y_rstd[u], 1)

            for t in range(HALVES // 4):
                for u in range(4):
                    row_powers(t, u)
                    if t + 1 < HALVES // 4:
                        scale_z2(pool, 1, t + 1, u)

        def window(t, p, k):
            nw = P // p
            return t[:, :, k:k + p * (nw - 1) + 1:p]

        @block.tensor
        def _(pe):
            mm = nc.tensor.matmul

            def keep_warm(bank, count):
                for _ in range(count):
                    mm(bank[:], s_hi[0][:, 0:P], s_hi[0][:], start=True, stop=True)

            pe.wait_ge(sem_zeros, 1)
            keep_warm(gate_bank[0][0], WARM_UP)
            pe.wait_ge(sem_adjT, 16)

            def emit(op, g, h):
                if op == ("lin0", "product", 0, 0) and isinstance(g, int) and (g, h) == (0, 0):
                    pe.wait_ge(sem_first, 16 * FIRST_LOADS)
                    mm(setup_bank[:, 0:P], bias0[:], adjT_sb[:], start=True, stop=True).then_inc(sem_setup_pe, 1)
                if isinstance(op[0], tuple):
                    lstm_product(op, g, h)
                elif op[0] == "back":
                    back_product(op, g, h)
                else:
                    front_product(op, g, h)
                if op == ("mix1", "product", 1, 3) and isinstance(g, int) and (g, h) == (0, 0):
                    pe.wait_ge(sem_setup, 2)
                    mm(setup_bank[:, 0:P], adj_sb[:], normed_sb[:, 1, P:2 * P], start=True, stop=True
                       ).then_inc(sem_setup_pe, 1)

            def front_product(op, g, h):
                stage, _, n, i = op
                b = 4 * n + i
                bank = front_to(g, h, n)
                cols = bank[:, i * P:(i + 1) * P]
                alone = not paired(g, h)
                if stage == "mix0":
                    if (n, i) == (0, 0):
                        pe.wait_ge(sem_x, loads(g, h))
                    if i == 0 and (n == 0 or not alone):
                        wait_earlier(pe, ("mix1", "out", 1 if alone else n), g, h, 1)
                    if (n, i) == (1, 0) and alone:
                        wait(pe, ("mix0", "out", 0), g, h)
                    ins = mm(cols, x_front[:, n, i * P:(i + 1) * P], adjT_sb[:], start=True, stop=True)
                elif stage == "lin0":
                    wait(pe, ("mix0", "out", 1 if alone else n), g, h)
                    if n == 1 and alone:
                        wait(pe, ("lin0", "biased", 0), g, h)
                    ins = mm(bank[:], w0_sb[:], mixed[:, n, :], start=True, stop=True)
                elif stage == "lin1":
                    if i == 0:
                        wait(pe, ("lin0", "out", n), g, h)
                        if alone:
                            wait(pe, ("lin0", "biased", 1) if n == 0 else ("lin1", "out", 0), g, h)
                    ins = mm(cols, flat(h0T[:])[:, b * P:(b + 1) * P], w1_sb[:], start=True, stop=True)
                else:
                    if i == 0:
                        wait(pe, ("lin1", "out", 1 if alone else n), g, h)
                        if n == 1 and alone:
                            wait(pe, ("mix1", "out", 0), g, h)
                    ins = mm(cols, flat(mixed[:])[:, b * P:(b + 1) * P], adjT_sb[:], start=True, stop=True)
                signal(ins, op, h)

            def back_product(op, g, h):
                _, what, n = op[0:3]
                bank = back_to(g, h, n)
                alone = not wide(g, h)
                if what == "tokens":
                    if (n, op[3]) == (0, 0):
                        wait(pe, (LSTM_JOBS[-1], "low"), g, h)
                        wait_earlier(pe, ("back", "z_stats", 3), g, h, 1)
                        if isinstance(g, int) and (g, h) == (0, 0):
                            wait(pe, ("mix1", "out", 1), (FRONT_PAIRED - 1) // 2, (FRONT_PAIRED - 1) % 2)
                    if (n, op[3]) == (1, 0) and alone:
                        wait(pe, ("back", "residual", 0), g, h)
                    for b in (2 * op[3], 2 * op[3] + 1):
                        to = bank[:, b * P:(b + 1) * P]
                        mm(to, h_hi[h][:, 4 * n + b, :], ident16[:], start=True, stop=False)
                        ins = mm(to, h_lo[h][:, 4 * n + b, :], ident16[:], start=False, stop=True)
                elif what == "mix":
                    i = op[3]
                    if (n, i) == (0, 0) and isinstance(g, int) and (g, h) == (GROUPS - 1, 1):
                        keep_warm(front_bank, STAY_WARM)
                    if i == 0:
                        wait(pe, ("back", "normed", n), g, h)
                        if n == 1 and alone:
                            wait(pe, ("back", "mixed_low", 0), g, h)
                    if i == 0 and n == 0:
                        pe.wait_ge(sem_ahat, 1)
                    ins = mm(bank[:, i * P:(i + 1) * P], normed[:, n, i * P:(i + 1) * P], ahatT[:],
                             start=True, stop=True)
                else:
                    if alone:
                        wait(pe, ("back", "z_stats", n - 1) if n else ("back", "mixed_low", 1), g, h)
                    else:
                        wait(pe, ("back", "mixed_low", min(n, 1)), g, h)
                    high, low = agg(n // 2)
                    mm(bank[:], gw1_hi[:, n % 2, :], high, start=True, stop=False)
                    mm(bank[:], gw1_lo[:, n % 2, :], high, start=False, stop=False)
                    ins = mm(bank[:], gw1_hi[:, n % 2, :], low, start=False, stop=True)
                signal(ins, op, h)

            def lstm_product(op, g, h):
                job, what, gate = op
                _, p, k = job
                to = gate_bank[h][bank_of(job, gate)]
                if p == 1:
                    if gate == "i":
                        wait(pe, ("mix1", "out", k), g, h)
                        if k == 0:
                            pe.wait_ge(sem_loaded, 16 * LOADS)
                            if isinstance(g, int) and (g, h) == (0, 1):
                                pe.wait_ge(sem_ahat, 1)
                            wait_earlier(pe, (LSTM_JOBS[-1], "act", "o"), g, h, 2)
                    if k == 1:
                        wait(pe, (LSTM_JOBS[0], "act", gate), g, h)
                    signal(mm(to[:], wih1_sb[:, GATES_FIRST.index(gate), :], h1T[:, k, :], start=True, stop=True),
                           op, h)
                    return
                s, n = p - SKIPS[0], columns_of(job)
                to = to[:, 0:n].rearrange("p (b w) -> p b w", b=GB)
                rows_at = slice(GATE_AT[gate] * P, (GATE_AT[gate] + 1) * P)
                w_in = w_hi[:, s, 0, rows_at], w_lo[:, s, 0, rows_at]
                w_rec = w_hi[:, s, 1, rows_at], w_lo[:, s, 1, rows_at]
                state = [t[h][:, 0:n].rearrange("p (b w) -> p b w", b=GB) for t in (s_hi, s_lo)]
                seen = [window(t[h], p, k) for t in (h_hi, h_lo)]
                prev = LSTM_JOBS[LSTM_JOBS.index(job) - 1]

                def high_part(w, v, start):
                    mm(to, w[0], v[0], start=start, stop=False)
                    mm(to, w[1], v[0], start=False, stop=False)

                if k == 0:
                    if gate == "i":
                        wait(pe, (prev, "low"), g, h)
                        if job == LSTM_JOBS[2]:
                            pe.wait_ge(sem_split, 1)
                    high_part(w_in, seen, True)
                    signal(mm(to, w_in[0], seen[1], start=False, stop=True), op, h)
                elif what == "input":
                    if gate == "o":
                        wait(pe, (job, "act", "i"), g, h)
                    else:
                        wait(pe, (prev, "act", bank_reader(prev, gate)), g, h)
                    high_part(w_in, seen, True)
                    mm(to, w_in[0], seen[1], start=False, stop=False)
                elif what == "high":
                    if gate == "i":
                        wait(pe, (prev, "high"), g, h)
                    high_part(w_rec, state, False)
                else:
                    if gate == "i":
                        wait(pe, (prev, "low"), g, h)
                    if gate in "fo":
                        high_part(w_rec, state, False)
                    signal(mm(to, w_rec[0], state[1], start=False, stop=True), op, h)

            run(pe, "PE", emit)

            keep_warm(front_bank, STAY_WARM)
            with pe.Fori(0, CHUNKS // TURN) as c:
                for m in range(TURN):
                    h = m % 2
                    pe.wait_ge(z2_kept[h], c * (TURN // 2) + (m // 2 + 1))
                    pe.wait_ge(r_ready[h], c * TURN + (m // 2 * 2 + 2))
                    for j in range(2):
                        last = mm(gate_bank[h][0][:], gw2_sb[:, j, :],
                                  z[:, bass.ds(c * TURN + m, 1), j, :].rearrange("p o n -> p (o n)"),
                                  start=(j == 0), stop=(j == 1))
                    last.then_inc(z2_full[h], 1)

            keep_warm(front_bank, STAY_WARM)
            pe.wait_ge(x1_back, 16 * HALVES)
            with pe.Fori(0, HALVES // 4) as t:
                for u in range(4):
                    pe.wait_ge(y_norm[u], t + 1)
                    for n in range(2):
                        to = row_bank[u][n]
                        pe.wait_ge(y_scaled[n][u], t + 1)
                        for b in range(4):
                            mm(to[:, b * P:(b + 1) * P], scaled[u][:, n, b * P:(b + 1) * P], ident[:],
                               start=(b == 0), stop=False, is_transpose=True, skip_group_check=True)
                        mm(to[:], ident[:], z[:, bass.ds(8 * t + (2 * u + n), 1), 1, :].rearrange("p o n -> p (o n)"),
                           start=False, stop=True, skip_group_check=True).then_inc(y_full[u], 1)

        @block.scalar
        def _(act):
            activation = nc.scalar.activation

            def emit(op, g, h):
                if isinstance(op[0], tuple):
                    job, what = op[0:2]
                    n = columns_of(job)
                    if what == "act":
                        gate = op[2]
                        p = job[1]
                        wait(act, (job, "gate", gate), g, h)
                        if gate == "i" and job == LSTM_JOBS[0]:
                            act.wait_ge(sem_setup, 1)
                        if gate == "o" and job == LSTM_JOBS[0]:
                            wait_earlier(act, (LSTM_JOBS[-1], "hidden"), g, h, 2)
                        if gate == "o" and job == LSTM_JOBS[1]:
                            wait(act, (LSTM_JOBS[0], "hidden"), g, h)
                        ins = activation(acts[gate][h][:, 0:n], gate_bank[h][bank_of(job, gate)][:, 0:n],
                                         ACT.Tanh if gate == "g" else ACT.Sigmoid,
                                         bias=lstm_bias[:, p - 1, GATE_AT[gate]:GATE_AT[gate] + 1],
                                         scale=1.0 if p == 1 else 1.0 / (W_SCALE * H_SCALE))
                    else:
                        wait(act, (job, "cell" if "f" in gates_of(job) else "new"), g, h)
                        ins = activation(acts["f"][h][:, 0:n], cell[h][:, 0:n], ACT.Tanh)
                elif op[0] == "back":
                    _, what, n = op
                    if what == "mixed":
                        wait(act, ("back", "mix", n, 3), g, h)
                        ins = activation(agg(n)[0], back_to(g, h, n)[:], ACT.Copy)
                    else:
                        wait(act, ("back", "z", n), g, h)
                        at = z[:, bass.ds(4 * g + (2 * h + n // 2), 1), n % 2, :].rearrange("p o n -> p (o n)")
                        ins = activation(at, back_to(g, h, n)[:], ACT.Identity, bias=v1_sb[:, 0, n % 2:n % 2 + 1],
                                         scale=1.0 / (W_SCALE * A_SCALE))
                else:
                    stage, _, n = op
                    if stage == "mix0":
                        wait(act, (stage, "product", n, 3), g, h)
                        ins = activation(mixed[:, n, :], front_to(g, h, n)[:], ACT.Copy)
                    elif stage == "lin0":
                        wait(act, (stage, "biased", n), g, h)
                        ins = activation(h0T[:, n, :], h0T[:, n, :], ACT.Relu)
                    else:
                        wait(act, (stage, "product", n, 3), g, h)
                        wait_earlier(act, (LSTM_JOBS[n], "gate", "o"), g, h, 1)
                        ins = activation(h1T[:, n, :], front_to(g, h, n)[:], ACT.Relu)
                signal(ins, op, h)

            run(act, "ACT", emit)

            wait(act, ("back", "z_stored", 3), GROUPS - 1, 1)
            act.wait_ge(sem_loaded, 16 * LOADS)
            act.wait_ge(sem_bn1, 5)
            with act.Fori(0, CHUNKS // 2) as c:
                for h in range(2):
                    for j in range(2):
                        at = z[:, bass.ds(2 * c + h, 1), j, :].rearrange("p o n -> p (o n)")
                        activation(at, at, ACT.Relu, bias=small[:, 10 + j:11 + j], scale=small[:, 8 + j:9 + j]
                                   ).then_inc(r_ready[h], 1)

            def normed_rows(t, u, last=False):
                act.wait_ge(y_shift[u], t + 1)
                for b in range(GB):
                    at = z[:, bass.ds(8 * t + (2 * u + b // 4), 1), 1, (b % 4) * P:(b % 4 + 1) * P]
                    ins = activation(at.rearrange("p o n -> p (o n)"),
                                     row_bank[u][b // 4][:, (b % 4) * P:(b % 4 + 1) * P], ACT.Identity,
                                     bias=mean_rstd[u][:, b:b + 1], scale=rstd[u][:, b:b + 1])
                    if last and b == 3:
                        ins.then_inc(y_last, 1)
                ins.then_inc(y_last if last else y_norm[u], 1)

            with act.Fori(0, HALVES // 4 - 1) as t:
                for u in range(4):
                    normed_rows(t, u)
            for u in range(4):
                normed_rows(HALVES // 4 - 1, u, u == 3)

        @block.vector
        def _(dve):
            ve = nc.vector
            ve.memset(s_hi[0][:], 0.0).then_inc(sem_zeros, 1)
            dve.wait_ge(sem_adjT, 16)
            dve.wait_ge(sem_first, 16 * FIRST_LOADS)
            dve.wait_ge(sem_ident, 3)
            scratch = normed_sb
            ve.tensor_copy(ident16[:], ident[:])
            ve.tensor_tensor(scratch[:, 0, 0:P], adj_sb[:], ident[:], ALU.mult)
            ve.tensor_tensor(scratch[:, 0, P:2 * P], adj_sb[:], adjT_sb[:], ALU.add)
            ve.tensor_tensor(adj_sb[:], adj_sb[:], ident[:], ALU.add).then_inc(sem_degree, 1)
            dve.wait_ge(sem_degree, 1)
            ve.tensor_tensor(scratch[:, 1, 0:P], scratch[:, 0, P:2 * P], scratch[:, 0, 0:P], ALU.subtract
                             ).then_inc(sem_degree, 1)
            dve.wait_ge(sem_degree, 2)
            ve.reduce_sum(small[:, 1:2], scratch[:, 1, 0:P], mybir.AxisListType.X).then_inc(sem_degree, 1)
            dve.wait_ge(sem_degree, 3)
            ve.tensor_scalar_add(small[:, 2:3], small[:, 1:2], 1.0).then_inc(sem_degree, 1)
            dve.wait_ge(sem_setup_pe, 1)
            ve.tensor_copy(bias0[:], setup_bank[:, 0:P]).then_inc(sem_degree, 1)
            dve.wait_ge(sem_loaded, 16 * LOADS)
            ve.tensor_tensor(lstm_bias[:], lstm_bias[:], bhh_sb[:], ALU.add).then_inc(sem_setup, 1)
            dve.wait_ge(sem_setup_pool, 1)
            ve.tensor_scalar(normed_sb[:, 1, P:2 * P], ident[:], small[:, 3:4], None, ALU.mult).then_inc(sem_setup, 1)
            dve.wait_ge(sem_degree, 5)

            def over4(t):
                return t[:].unsqueeze(1).broadcast_to([P, 4, P])

            def prepare_back():
                dve.wait_ge(sem_wr, 16)
                ve.tensor_scalar(w_hi[:], w_stage, W_SCALE, None, ALU.mult).then_inc(sem_degree, 1)
                dve.wait_ge(sem_degree, 6)
                for s in range(3):
                    for m in range(2):
                        ve.scalar_tensor_tensor(out=w_lo[:, s, m, :], in0=w_stage[:, s, m, :], scalar=W_SCALE,
                                                in1=w_hi[:, s, m, :], op0=ALU.mult, op1=ALU.subtract)
                ve.tensor_scalar(gw1_hi[:], gw1_stage, W_SCALE, None, ALU.mult).then_inc(sem_degree, 1)
                dve.wait_ge(sem_degree, 7)
                ve.scalar_tensor_tensor(out=gw1_lo[:], in0=gw1_stage, scalar=W_SCALE, in1=gw1_hi[:], op0=ALU.mult,
                                        op1=ALU.subtract).then_inc(sem_split, 1)
                dve.wait_ge(sem_setup_pe, 2)
                ve.tensor_scalar(ahatT[:], setup_bank[:, 0:P], small[:, 3:4], A_SCALE, ALU.mult, ALU.mult).then_inc(sem_ahat, 1)

            def emit(op, g, h):
                if isinstance(op[0], tuple):
                    lstm_state(op, g, h)
                elif op[0] == "back":
                    back_rows(op, g, h)
                else:
                    stage, _, n = op
                    wait(dve, (stage, "product", n, 0 if stage == "lin0" else 3), g, h)
                    dst, bias = (h0T, bias0) if stage == "lin0" else (mixed, bias1)
                    signal(ve.tensor_tensor(dst[:, n, :].rearrange("p (b n) -> p b n", n=P),
                                            front_to(g, h, n)[:].rearrange("p (b n) -> p b n", n=P), over4(bias), ALU.add),
                           op, h)
                    if op == ("lin1", "out", 1) and isinstance(g, int) and (g, h) == (0, 0):
                        prepare_back()

            def row_stats(t, bn_t, n):
                for b in range(4):
                    last = ve.bn_stats(bn_t[:, 4 * n + b, :], t[:, b * P:(b + 1) * P])
                return last

            def row_moments(bn_t, comb_t, veps_t, step):
                mean_e, m2_e, mean_o, m2_o = (bn_t[:, :, n] for n in (1, 2, 4, 5))
                apart, m2, mean = (comb_t[:, n, :] for n in range(3))
                if step == 0:
                    ve.tensor_tensor(apart, mean_e, mean_o, ALU.subtract)
                    ve.scalar_tensor_tensor(out=m2, in0=m2_e, scalar=P * EPS, in1=m2_o, op0=ALU.add, op1=ALU.add)
                    return ve.tensor_tensor(mean, mean_e, mean_o, ALU.add)
                if step == 1:
                    ve.tensor_scalar(mean, mean, 0.5, None, ALU.mult)
                    return ve.scalar_tensor_tensor(out=apart, in0=apart, scalar=0.25, in1=apart, op0=ALU.mult,
                                                   op1=ALU.mult)
                return ve.scalar_tensor_tensor(out=veps_t[:], in0=m2, scalar=1.0 / P, in1=apart, op0=ALU.mult,
                                               op1=ALU.add)

            def normalize(src, dst, comb_t, rstd_t, n):
                for b in range(4 * n, 4 * n + 4):
                    at = slice(b * P, (b + 1) * P)
                    last = ve.tensor_scalar(flat(dst[:])[:, at], flat(src[:])[:, at], comb_t[:, 2, b:b + 1],
                                            rstd_t[:, b:b + 1], ALU.subtract, ALU.mult)
                return last

            def back_rows(op, g, h):
                _, what, n = op
                if what == "residual":
                    wait(dve, ("back", "tokens", n, 1), g, h)
                    if n == 0:
                        dve.wait_ge(sem_xb, loads(g, h))
                    ins = ve.scalar_tensor_tensor(out=rows[:, n, :], in0=back_to(g, h, n)[:], scalar=1.0 / H_SCALE,
                                                  in1=rows[:, n, :], op0=ALU.mult, op1=ALU.add)
                elif what == "stats":
                    wait(dve, ("back", "residual", n), g, h)
                    ins = row_stats(rows[:, n, :], bn[0], n)
                elif what == "moments":
                    wait(dve, ("back", "moments", n - 1) if n else ("back", "stats", 1), g, h)
                    ins = row_moments(bn[0], comb[0], veps[0], n)
                elif what == "normed":
                    if n == 0:
                        wait(dve, ("back", "rstd"), g, h)
                        if isinstance(g, int):
                            if 2 * g + h > 0:
                                dve.wait_ge(sem_kept, 16 * (2 * g + h))
                        else:
                            dve.wait_ge(sem_kept, loads(g, h, -16))
                    ins = normalize(rows, normed, comb[0], rstd[0], n)
                elif what == "mixed_low":
                    wait(dve, ("back", "mixed", n), g, h)
                    high, low = agg(n)
                    ins = ve.tensor_tensor(low, back_to(g, h, n)[:], high, ALU.subtract)
                else:
                    wait(dve, ("back", "z_stored", n), g, h)
                    at = z_moments[:, n % 2, bass.ds(4 * g + (2 * h + n // 2), 1), :].rearrange("p o s -> p (o s)")
                    ins = ve.bn_stats(at, back_to(g, h, n)[:])
                signal(ins, op, h)

            def lstm_state(op, g, h):
                job, what = op
                _, p, k = job
                n = columns_of(job)
                i, gg, f, o = (acts[name][h][:, 0:n] for name in "igfo")
                c = cell[h][:, 0:n]
                if what == "new":
                    wait(dve, (job, "act", "g"), g, h)
                    ins = ve.tensor_tensor(i if "f" in gates_of(job) else c, i, gg, ALU.mult)
                elif what == "kept":
                    wait(dve, (job, "act", "f"), g, h)
                    ins = ve.tensor_tensor(c, c, f, ALU.mult)
                elif what == "cell":
                    wait(dve, (job, "kept"), g, h)
                    ins = ve.tensor_tensor(c, c, i, ALU.add)
                elif what == "hidden":
                    wait(dve, (job, "tanh"), g, h)
                    ins = ve.scalar_tensor_tensor(out=f, in0=o, scalar=H_SCALE, in1=f, op0=ALU.mult, op1=ALU.mult)
                else:
                    if p == 1:
                        hi, lo = (t[h][:, 4 * k:4 * k + 4, :].rearrange("p b t -> p (b t)") for t in (h_hi, h_lo))
                    elif k < p - 1:
                        hi, lo = s_hi[h][:, 0:n], s_lo[h][:, 0:n]
                    else:
                        hi, lo = window(h_hi[h], p, k), window(h_lo[h], p, k)
                        f = f.rearrange("p (b w) -> p b w", b=GB)
                    if what == "high":
                        wait(dve, (job, "hidden"), g, h)
                        if job == LSTM_JOBS[0]:
                            wait_earlier(dve, ("back", "tokens", 1, 1), g, h, 2)
                        ins = ve.tensor_copy(hi, f)
                    else:
                        wait(dve, (job, "high"), g, h)
                        ins = ve.tensor_tensor(lo, f, hi, ALU.subtract)
                signal(ins, op, h)

            run(dve, "DVE", emit)

            wait(dve, ("back", "z_stats", 3), GROUPS - 1, 1)
            for j in range(2):
                last = ve.bn_aggr(mv[:, j, :], z_moments[:, j, :, :].rearrange("p c s -> p (c s)"))
            last.then_inc(sem_bn1, 1)
            dve.wait_ge(sem_bn1, 1)
            scale = 1.0 / (W_SCALE * A_SCALE)
            ve.scalar_tensor_tensor(out=small[:, 14:16], in0=mv[:, 0:2, 0], scalar=scale, in1=v1_sb[:, 0, :],
                                    op0=ALU.mult, op1=ALU.add)
            ve.tensor_scalar(small[:, 4:6], mv[:, 0:2, 1], scale ** 2, EPS, ALU.mult, ALU.add).then_inc(sem_bn1, 1)
            dve.wait_ge(sem_bn1_pow, 1)
            ve.tensor_tensor(small[:, 8:10], small[:, 6:8], v1_sb[:, 1, :], ALU.mult).then_inc(sem_bn1, 1)
            dve.wait_ge(sem_bn1, 3)
            ve.tensor_tensor(small[:, 14:16], small[:, 14:16], small[:, 8:10], ALU.mult).then_inc(sem_bn1, 1)
            dve.wait_ge(sem_bn1, 4)
            ve.tensor_tensor(small[:, 10:12], v1_sb[:, 2, :], small[:, 14:16], ALU.subtract).then_inc(sem_bn1, 1)

            with dve.Fori(0, CHUNKS // 2) as c:
                for h in range(2):
                    dve.wait_ge(z2_full[h], c + 1)
                    ve.bn_stats(z_moments[:, 0, bass.ds(2 * c + h, 1), :].rearrange("p o s -> p (o s)"),
                                gate_bank[h][0][:])
                    ve.tensor_scalar(z[:, bass.ds(2 * c + h, 1), 0, :].rearrange("p o n -> p (o n)"),
                                     gate_bank[h][0][:], v2_sb[:, 0:1], None, ALU.add).then_inc(z2_kept[h], 1)

            for h in range(2):
                dve.wait_ge(z2_kept[h], CHUNKS // 2 + 1)
            ve.bn_aggr(mv[:, 0, :], z_moments[:, 0, :, :].rearrange("p c s -> p (c s)")).then_inc(sem_bn2, 1)
            dve.wait_ge(sem_bn2, 1)
            ve.tensor_tensor(small[:, 14:15], mv[:, 0, 0:1], v2_sb[:, 0:1], ALU.add)
            ve.tensor_scalar_add(small[:, 12:13], mv[:, 0, 1:2], EPS).then_inc(sem_bn2, 1)
            dve.wait_ge(sem_bn2_pow, 1)
            ve.tensor_tensor(small[:, 1:2], small[:, 13:14], v2_sb[:, 1:2], ALU.mult).then_inc(sem_bn2, 1)
            dve.wait_ge(sem_bn2, 3)
            ve.tensor_tensor(small[:, 15:16], small[:, 14:15], small[:, 1:2], ALU.mult).then_inc(sem_bn2, 1)
            dve.wait_ge(sem_bn2, 4)
            ve.tensor_tensor(small[:, 2:3], v2_sb[:, 2:3], small[:, 15:16], ALU.subtract).then_inc(sem_bn2, 1)

            def row_terms(t, u, between):
                for n in range(2):
                    dve.wait_ge(y_full[u], 2 * t + n + 2)
                    last = row_stats(row_bank[u][n], bn[u], n)
                last.then_inc(y_mom[u], 1)
                for step in range(3):
                    dve.wait_ge(y_mom[u], 4 * t + step + 1)
                    row_moments(bn[u], comb[u], veps[u], step).then_inc(y_mom[u], 1)
                    between[step]()

            def row_shift(t, u):
                dve.wait_ge(y_rstd[u], t + 1)
                ve.scalar_tensor_tensor(out=mean_rstd[u][:], in0=comb[u][:, 2, :], scalar=-1.0, in1=rstd[u][:],
                                        op0=ALU.mult, op1=ALU.mult).then_inc(y_shift[u], 1)

            def four_rows(t, first, last):
                def nothing():
                    pass

                for u in range(4):
                    scale = nothing if last else lambda: scale_z2(dve, 0, t + 1, u)
                    if u:
                        shift = lambda: row_shift(t, u - 1)
                    else:
                        shift = nothing if first else lambda: row_shift(t - 1, 3)
                    row_terms(t, u, (shift, scale, nothing))

            dve.wait_ge(sem_bn2, 5)
            for u in range(4):
                scale_z2(dve, 0, 0, u)
            LAST = HALVES // 4 - 1
            four_rows(0, True, False)
            with dve.Fori(1, LAST) as t:
                four_rows(t, False, False)
            four_rows(LAST, False, True)
            row_shift(LAST, 3)
        return nc


INPUTS = ("x", "adj", "adjT", "w0", "b0_rep", "w1", "b1_rep", "wih1", "b_ih", "b_hh", "wr", "gw1", "gw2",
          "vec1", "vec2")


def kernel(**inputs):
    import concourse.bacc as bacc
    from concourse.bass_utils import run_bass_kernel_spmd

    a = {k: np.asarray(v) for k, v in inputs.items()}
    x = a["x"]
    nb = x.shape[0]
    wih, whh = a["L0_gnn_Wih"], a["L0_gnn_Whh"]
    laid = {
        "x": x.reshape(nb // GB, GB, P, P).transpose(0, 2, 1, 3).reshape(nb // GB, P, GB * P),
        "adj": a["adj"],
        "adjT": a["adj"].T,
        "w0": a["L0_gnn_Wg0"],
        "b0_rep": np.broadcast_to(a["L0_gnn_bg0"][None, :], (P, P)),
        "w1": a["L0_gnn_Wg1"],
        "b1_rep": np.broadcast_to(a["L0_gnn_bg1"][None, :], (P, P)),
        "wih1": np.stack([wih[0, GATE_AT[n] * P:(GATE_AT[n] + 1) * P].T for n in GATES_FIRST], axis=1),
        "b_ih": a["L0_gnn_bih"].reshape(4, 4, P).transpose(2, 0, 1),
        "b_hh": a["L0_gnn_bhh"].reshape(4, 4, P).transpose(2, 0, 1),
        "wr": np.stack([wih[1:], whh[1:]], axis=1).transpose(3, 0, 1, 2),
        "gw1": a["L1_gnn_W1"].reshape(2, P, P).transpose(2, 0, 1),
        "gw2": a["L1_gnn_W2"].reshape(P, 2, P).transpose(2, 1, 0),
        "vec1": np.stack([a[f"L1_gnn_{n}"].reshape(2, P).T for n in ("b1", "g1", "be1")], axis=1),
        "vec2": np.stack([a[f"L1_gnn_{n}"] for n in ("b2", "g2", "be2")], axis=1),
    }
    nc = bacc.Bacc("TRN2", target_bir_lowering=False, num_devices=1)
    arrays, args = {}, []
    for name in INPUTS:
        arrays[f"in_{name}"] = np.ascontiguousarray(laid[name])
        args.append(nc.dram_tensor(f"in_{name}", arrays[f"in_{name}"].shape, F32, kind="ExternalInput").ap())
    out = nc.dram_tensor("out", (nb // GB, P, GB * P), F32, kind="ExternalOutput").ap()
    gnn_lstm_kernel(nc, *args, out)
    result = run_bass_kernel_spmd(nc, [arrays], core_ids=[0]).results[0]["out"]
    return result.reshape(nb // GB, P, GB, P).transpose(0, 2, 1, 3).reshape(nb, P, P)
```
